# Optimizing a Trainium2 kernel written in Bass

```python
import numpy as np
import jax
import jax.numpy as jnp

def _softmax(x, axis=-1):
    return jax.nn.softmax(x, axis=axis)

def _gelu(x):
    return jax.nn.gelu(x, approximate=True)

def _silu(x):
    return jax.nn.silu(x)

def _sigmoid(x):
    return jax.nn.sigmoid(x)

def _layernorm(x, axis=-1, eps=1e-05):
    m = jnp.mean(x, axis=axis, keepdims=True)
    v = jnp.var(x, axis=axis, keepdims=True)
    return (x - m) / jnp.sqrt(v + eps)

def _scatter_add(tgt, idx, src, axis=0):
    return tgt.at[idx].add(src)

def _segment_sum(src, seg, n):
    return jax.ops.segment_sum(src, seg, n)
kernel_name = 'mk_seq_preln_d1_jaxref_r4_9e9750'

def setup_inputs(seed: int=0):
    np.random.seed(seed)
    _w = jnp.asarray

    def _L0_attn_setup():
        import jax, jax.numpy as jnp
        import numpy as np
        EPS = 1e-08

        def rms_norm_multihead(x, weight):
            x32 = x.astype(jnp.float32)
            normed = x32 * jax.lax.rsqrt(jnp.mean(x32 * x32, axis=-1, keepdims=True) + EPS)
            return normed.astype(x.dtype) * weight
        key = jax.random.key(seed)
        k0, k1, k2 = jax.random.split(key, 3)
        B, L, D, H = (2, 256, 256, 16)
        d = D // H
        X = jax.random.normal(k0, (B, L, D), dtype=jnp.float32)
        Wq = jax.random.normal(k1, (D, D), dtype=jnp.float32) * 0.02
        Wv = jax.random.normal(k2, (D, D), dtype=jnp.float32) * 0.02
        q_norm_w = jnp.ones((H, d), dtype=jnp.float32)
        v_norm_w = jnp.ones((H, d), dtype=jnp.float32)
        return {'X': X, 'Wq': Wq, 'Wv': Wv, 'q_norm_w': q_norm_w, 'v_norm_w': v_norm_w}
    _L0_attn_in = _L0_attn_setup()

    def _L0_ffn_setup():
        import jax, jax.numpy as jnp
        import numpy as np
        TOP_K = 4
        CAP_FACTOR = 4

        def swiglu(x, w1, w2, w3):
            return jax.nn.silu(x @ w1) * (x @ w3) @ w2
        key = jax.random.key(seed)
        ks = jax.random.split(key, 8)
        B, S, D, H, E = (2, 512, 256, 128, 32)
        Hs = 2 * H
        sd = lambda *sh: 1.0 / np.sqrt(sh[-2])
        x = jax.random.normal(ks[0], (B, S, D), dtype=jnp.float32)
        Wg = jax.random.normal(ks[1], (D, E), dtype=jnp.float32) * (1.0 / np.sqrt(D))
        W1 = jax.random.normal(ks[2], (E, D, H), dtype=jnp.float32) * (1.0 / np.sqrt(D))
        W3 = jax.random.normal(ks[3], (E, D, H), dtype=jnp.float32) * (1.0 / np.sqrt(D))
        W2 = jax.random.normal(ks[4], (E, H, D), dtype=jnp.float32) * (1.0 / np.sqrt(H))
        Ws1 = jax.random.normal(ks[5], (D, Hs), dtype=jnp.float32) * (1.0 / np.sqrt(D))
        Ws3 = jax.random.normal(ks[6], (D, Hs), dtype=jnp.float32) * (1.0 / np.sqrt(D))
        Ws2 = jax.random.normal(ks[7], (Hs, D), dtype=jnp.float32) * (1.0 / np.sqrt(Hs))
        return {'x': x, 'Wg': Wg, 'W1': W1, 'W2': W2, 'W3': W3, 'Ws1': Ws1, 'Ws2': Ws2, 'Ws3': Ws3}
    _L0_ffn_in = _L0_ffn_setup()
    _d = {'L0_attn_X': _L0_attn_in['X'], 'L0_attn_Wq': _L0_attn_in['Wq'], 'L0_attn_Wv': _L0_attn_in['Wv'], 'L0_attn_q_norm_w': _L0_attn_in['q_norm_w'], 'L0_attn_v_norm_w': _L0_attn_in['v_norm_w'], 'L0_ffn_Wg': _L0_ffn_in['Wg'], 'L0_ffn_W1': _L0_ffn_in['W1'], 'L0_ffn_W2': _L0_ffn_in['W2'], 'L0_ffn_W3': _L0_ffn_in['W3'], 'L0_ffn_Ws1': _L0_ffn_in['Ws1'], 'L0_ffn_Ws2': _L0_ffn_in['Ws2'], 'L0_ffn_Ws3': _L0_ffn_in['Ws3']}
    _x0 = _d['L0_attn_X']
    _d['L0_attn_X'] = jax.random.normal(jax.random.fold_in(jax.random.key(seed), 1), (2, 2048, 256), dtype=_x0.dtype)
    del _x0
    return _d

def reference(L0_attn_X, L0_attn_Wq, L0_attn_Wv, L0_attn_q_norm_w, L0_attn_v_norm_w, L0_ffn_Wg, L0_ffn_W1, L0_ffn_W2, L0_ffn_W3, L0_ffn_Ws1, L0_ffn_Ws2, L0_ffn_Ws3):

    def _L0_attn_ref(X, Wq, Wv, q_norm_w, v_norm_w):
        import jax, jax.numpy as jnp
        import numpy as np
        EPS = 1e-08

        def rms_norm_multihead(x, weight):
            x32 = x.astype(jnp.float32)
            normed = x32 * jax.lax.rsqrt(jnp.mean(x32 * x32, axis=-1, keepdims=True) + EPS)
            return normed.astype(x.dtype) * weight
        B, L, D = X.shape
        H, d = q_norm_w.shape
        K = X.reshape(B, L, H, d)
        Q = rms_norm_multihead((X @ Wq.T).reshape(B, L, H, d), q_norm_w)
        V = rms_norm_multihead((X @ Wv.T).reshape(B, L, H, d), v_norm_w)
        W = jnp.cumsum(jnp.einsum('blhd,blhe->blhde', K, V), axis=1)
        out = jnp.einsum('blhd,blhde->blhe', Q, W).reshape(B, L, D)
        return out

    def _L0_ffn_ref(x, Wg, W1, W2, W3, Ws1, Ws2, Ws3):
        import jax, jax.numpy as jnp
        import numpy as np
        TOP_K = 4
        CAP_FACTOR = 4

        def swiglu(x, w1, w2, w3):
            return jax.nn.silu(x @ w1) * (x @ w3) @ w2
        B, S, D = x.shape
        E = Wg.shape[1]
        T = B * S
        xf = x.reshape(T, D)
        scores = jax.nn.softmax(xf @ Wg, axis=-1)
        weights, indices = jax.lax.top_k(scores, TOP_K)
        P = T * TOP_K
        pair_expert = indices.reshape(-1)
        pair_token = jnp.repeat(jnp.arange(T), TOP_K)
        pair_weight = weights.reshape(-1).astype(xf.dtype)
        C = CAP_FACTOR * P // E
        y = jnp.zeros_like(xf)
        for e in range(E):
            pos = jnp.nonzero(pair_expert == e, size=C, fill_value=P)[0]
            valid = pos < P
            safe = jnp.minimum(pos, P - 1)
            tok = jnp.where(valid, pair_token[safe], 0)
            w = jnp.where(valid, pair_weight[safe], 0.0)
            xg = xf[tok]
            out = swiglu(xg, W1[e], W2[e], W3[e]) * w[:, None]
            y = y.at[tok].add(out)
        z = swiglu(xf, Ws1, Ws2, Ws3)
        return (y + z).reshape(B, S, D)
    x = L0_attn_X
    x = x + _L0_attn_ref(_layernorm(x, axis=-1), L0_attn_Wq, L0_attn_Wv, L0_attn_q_norm_w, L0_attn_v_norm_w)
    x = x + _L0_ffn_ref(_layernorm(x, axis=-1), L0_ffn_Wg, L0_ffn_W1, L0_ffn_W2, L0_ffn_W3, L0_ffn_Ws1, L0_ffn_Ws2, L0_ffn_Ws3)
    return x

_drawn_inputs = setup_inputs


def setup_inputs(seed=0):
    import zlib

    import numpy as np

    out = dict(_drawn_inputs(seed))
    spreads = {'L0_attn_q_norm_w': (1.0, 0.2), 'L0_attn_v_norm_w': (1.0, 0.2)}
    factors = {'L0_ffn_Wg': 8.0,
     'L0_ffn_W1': 8.0,
     'L0_ffn_W2': 8.0,
     'L0_ffn_W3': 8.0,
     'L0_ffn_Ws1': 8.0,
     'L0_ffn_Ws2': 8.0,
     'L0_ffn_Ws3': 8.0}
    for name, (base, spread) in spreads.items():
        noise = np.random.default_rng([zlib.crc32(name.encode()), seed]).standard_normal(out[name].shape)
        drawn = base * np.exp(spread * noise) if base else spread * noise
        out[name] = jnp.asarray(drawn.astype(out[name].dtype))
    for name, factor in factors.items():
        out[name] = (out[name] * factor).astype(out[name].dtype)
    return out
```

```python
from contextlib import ExitStack

import concourse.bass as bass
from concourse import mybir

F32 = mybir.dt.float32
BF16 = mybir.dt.bfloat16
I32 = mybir.dt.int32
U32 = mybir.dt.uint32
ALU = mybir.AluOpType
ACT = mybir.ActivationFunctionType
AX_X = mybir.AxisListType.X

P = 128
LN_EPS = 1e-5
RMS_EPS = 1e-8
TOP_K = 4
CAP_FACTOR = 4


class Tile:

    def __init__(self, t, ring):
        self.t, self.ring = t, ring
        self.b = ring % 2


def pipelined(eng, n, unroll, lead, depth, step):
    def peeled(i):
        def tile_of(skew):
            return Tile(i - skew, (i - skew) % 4) if 0 <= i - skew < n else None
        step(tile_of)

    def looped(r, k):
        def tile_of(skew):
            return Tile(r * unroll + (k - skew), (k - skew) % unroll if unroll == 4 else (k - skew) % 2)
        step(tile_of)

    assert lead % unroll == 0 and n % unroll == 0
    for i in range(lead):
        peeled(i)
    with eng.Fori(lead // unroll, n // unroll) as r:
        for k in range(unroll):
            looped(r, k)
    for i in range(n, n + depth):
        peeled(i)


def wait(eng, sem, count, most=None):
    if isinstance(count, int):
        if count <= 0:
            return
        if most is not None:
            count = min(count, most)
    eng.wait_ge(sem, count)


def wait_at_ends(eng, sem, count, most=None):
    if isinstance(count, int):
        wait(eng, sem, count, most)


def build(nc, X, Wq, Wv, q_norm_w, v_norm_w, Wg, W1, W2, W3, Ws1, Ws2, Ws3, out):
    B, L, D = X.shape
    H, d = q_norm_w.shape
    E = Wg.shape[1]
    F = W1.shape[2]
    FS = Ws1.shape[1]
    T = B * L
    NT = T // P
    NTB = L // P
    KC = D // P
    FC = FS // P
    PAIRS = T * TOP_K
    CAP = CAP_FACTOR * PAIRS // E
    NBE = T // P
    NB = E * NBE
    NJ = PAIRS // P + E
    HG = P // d
    NP_ = H // 2
    TG = 512
    NG = T // TG
    assert D == 256 and d == 16 and F == 128 and FS == 256 and E == 32

    ctx = ExitStack()
    with ctx:
        def sb(name, shape, dt=F32):
            return ctx.enter_context(nc.sbuf_tensor(name, shape, dt))

        def pb(name):
            return ctx.enter_context(nc.psum_tensor(name, [P, 512], F32))

        def sem(name):
            return ctx.enter_context(nc.semaphore(name))

        xn2_rows = nc.dram_tensor("xn2_rows", [T, D], F32).ap()
        lists = nc.dram_tensor("lists", [(NB + 1) * P, 1], F32).ap()
        pair_rows = nc.dram_tensor("pair_rows", [PAIRS, D], F32).ap()
        lists_blocks = lists.rearrange("(b r) o -> b (r o)", r=P)

        x_tiles = X.rearrange("b (t p) c -> p (b t) c", p=P)
        out_tiles = out.rearrange("b (t p) c -> (b t) p c", p=P)

        xall = sb("xall", [P, NT, D])
        x2T_all = sb("x2T_all", [P, KC, T])
        w13 = sb("w13", [P, E, KC, 2, F])
        w2 = sb("w2", [P, E, D])
        ws13 = sb("ws13", [P, KC, 2, FS])
        ws2 = sb("ws2", [P, FC, D])
        ident = sb("ident", [P, P])
        tri = sb("tri", [P, P])
        keep = sb("keep", [P, NT + 2])
        wqc = sb("wqc", [P, KC])
        wvc = sb("wvc", [P, KC])
        wg = sb("wg", [P, KC, E])
        par_i = sb("par_i", [P, 1], I32)
        par_f = sb("par_f", [P, 2])
        mwq = sb("mwq", [P, 2, KC])
        head_mask = sb("head_mask", [P, KC, P])
        tri_bf = sb("tri_bf", [P, P], BF16)
        ones_bf = sb("ones_bf", [P, P], BF16)
        eidx_i = sb("eidx_i", [P, E], I32)
        eidx = sb("eidx", [P, E])
        ebase = sb("ebase", [P, E])
        pair_i = sb("pair_i", [P, NT * TOP_K], I32)
        pair_all = sb("pair_all", [P, NT, TOP_K])

        st = sb("st", [P, 6])
        mv1 = sb("mv1", [P, 2, 2])
        rs1 = sb("rs1", [P, 2])
        st2 = sb("st2", [P, 6])
        mv2 = sb("mv2", [P, 2, 2])
        rs2 = sb("rs2", [P, 2])
        ss = sb("ss", [P, 2, 2 * H])
        rr = sb("rr", [P, 2, 2 * H])
        var1 = sb("var1", [P, 1])
        var2 = sb("var2", [P, 1])
        minus_half = sb("minus_half", [P, 1])
        eps_col = sb("eps_col", [P, 1])
        lnm = sb("lnm", [P, 2 * H])
        guess = sb("guess", [P, 2 * H])
        msq = sb("msq", [P, 2 * H])
        gg = sb("gg", [P, 2 * H])
        mgg = sb("mgg", [P, 2 * H])
        fac = sb("fac", [P, 2 * H])
        w_raw = sb("w_raw", [P, KC * P])
        w_bd = sb("w_bd", [P, 2, KC * P])
        lg = sb("lg", [P, 2, E])
        m8 = sb("m8", [P, 8])
        nmx = sb("nmx", [P, 2])
        ex = sb("ex", [P, 2, E])
        se = sb("se", [P, 2])
        rin = sb("rin", [P, 1])
        prob = sb("prob", [P, E])
        t8 = sb("t8", [P, 8])
        ix = sb("ix", [P, 8], U32)
        ixf = sb("ixf", [P, TOP_K])
        oh = sb("oh", [P, TOP_K, E])
        ohr = sb("ohr", [P, TOP_K, E])
        mask = sb("mask", [P, 2, E], BF16)
        mcum = sb("mcum", [P, 2, E], BF16)
        place = sb("place", [P, E])
        pos = sb("pos", [P, TOP_K])
        posi = sb("posi", [P, 2, TOP_K], I32)
        pid = sb("pid", [P, 2, TOP_K])
        posi_all = sb("posi_all", [P, NT, TOP_K], I32)
        wts = sb("wts", [P, NT, TOP_K])

        arena = w2[:].rearrange("p e c -> p (e c)")
        cut = [0]

        def part(width):
            cut[0] += width
            assert cut[0] <= E * D
            return arena[:, cut[0] - width:cut[0]]

        s_sb = part(2048).rearrange("p (j g r l) -> p j g r l", j=4, g=2, r=2)
        sq = part(512)
        qm = part(512).rearrange("p (r g l) -> p r g l", r=2, g=2)
        qn = part(512).rearrange("p (b c) -> p b c", b=2)
        qT = part(256).rearrange("p (g l) -> p g l", g=2)
        vp = part(2 * NP_ * 3 * d).rearrange("p (b n k e) -> p b n k e", b=2, n=NP_, k=3)
        xn = part(512).rearrange("p (b c) -> p b c", b=2)
        xnT = part(512).rearrange("p (b g m) -> p b g m", b=2, g=2)
        oT = part(512).rearrange("p (b g l) -> p b g l", b=2, g=2)
        xn2 = part(512).rearrange("p (b c) -> p b c", b=2)
        x2T = part(512).rearrange("p (b g l) -> p b g l", b=2, g=2)
        wqv = part(KC * 512).rearrange("p (k c) -> p k c", k=KC)
        A_END = cut[0]
        wq_in = s_sb.rearrange("p j g r l -> p (j g r l)")[:, 0:512].rearrange("p (k c) -> p k c", k=2)
        wv_in = s_sb.rearrange("p j g r l -> p (j g r l)")[:, 512:1024].rearrange("p (k c) -> p k c", k=2)

        sg = sb("sg", [P, FC, TG])
        gsh = sb("gsh", [P, 2, FC, TG])
        pad = gsh[:].rearrange("p b f t -> p (b f t)")[:, 0:NB + 1]
        xg = sb("xg", [P, 4, D])
        after_s = gsh[:].rearrange("p b f t -> p (b f t)")
        xgT = after_s[:, 0:512].rearrange("p (b g m) -> p b g m", b=2, g=KC)
        sge = after_s[:, 512:768].rearrange("p (b f) -> p b f", b=2)
        ge = after_s[:, 768:1024].rearrange("p (b f) -> p b f", b=2)
        geT = after_s[:, 1024:1280].rearrange("p (b f) -> p b f", b=2)
        y = sg[:].rearrange("p f t -> p (f t)").rearrange("p (b c) -> p b c", b=4)
        rows = gsh[:].rearrange("p b f t -> p b (f t)").rearrange("p b (k c) -> p b k c", k=TOP_K)
        cnt_i = sb("cnt_i", [P, E], I32)
        nt_i = sb("nt_i", [P, E], I32)
        ntf = sb("ntf", [P, E])
        ones_f = sb("ones_f", [P, E])
        endt = sb("endt", [P, E])
        jc_i = sb("jc_i", [P, 2], I32)
        jc = sb("jc", [P, 2])
        behind = sb("behind", [P, 2, E])
        ej = sb("ej", [P, 2])
        bnt = sb("bnt", [P, 2, E])
        stj = sb("stj", [P, 2])
        jrel = sb("jrel", [P, 2])
        blk = sb("blk", [P, 2])
        blk_i = sb("blk_i", [P, 2], I32)
        ejc = sb("ejc", [P, 2])
        erow = sb("erow", [1, 256], I32)
        lj = sb("lj", [P, 2, P])
        slot_i = sb("slot_i", [P, NJ], I32)
        tok_i = sb("tok_i", [P, NJ], I32)
        tok_b = sb("tok_b", [P, 4], I32)
        slot_b = sb("slot_b", [P, 4], I32)
        rank_i = sb("rank_i", [P, NT * TOP_K], I32)
        inside = sb("inside", [P, NT * TOP_K])

        pT0, pT1, pQV, pO = pb("pT0"), pb("pT1"), pb("pQV"), pb("pO")
        pS = [pb(f"pS{j}") for j in range(4)]

        names = """var1_done var2_done ln_done guess_done msq_done gg_done mgg_done fac_done x_first x_rest w_in wc_in wg_in consts_pool consts_dve wt_ps wt_done
            stats1 mean1 rstd1 xn_done xnT_ps xnT_done qv_ps sq_done ss_done rms_done qn_done v_done
            qT_ps qm_done qT_done scores_ps masked state_ps raw_done state_done o_ps oT_done
            ot_ps x2_done stats2 mean2 rstd2 xn2_done x2T_ps x2T_done x2T_kept logits_ps
            lg_done max_done nmx_done exp_done rin_done prob_done top_done ix_done ixf_done oh_done mask_done
            mcum_done rank_ps place_done placed_done pos_done pos_kept pid_done lists_padded
            w13_in w2_in ws_in h_ps silu_done gsh_done z_ps z_done
            cnt_ps tabs tab_blk tab_lj_in tab_ps tab_done erow_ps erow_done ridx_ps
            bcopy xT_ps xT_done hb_ps sge_done ge_done gT_ps gT_done y_ps y_done wt_kept""".split()
        S = {n: sem(n) for n in names}
        stored = [sem(f"stored{b}") for b in range(2)]
        scattered = [sem(f"scattered{b}") for b in range(2)]
        gathered = [sem(f"gathered{b}") for b in range(4)]
        put = [sem(f"put{b}") for b in range(4)]
        rows_in = [sem(f"rows_in{b}") for b in range(2)]
        summed = sem("summed")
        passed = {e.engine: sem(n) for n, e in (("passed_pool", nc.gpsimd), ("passed_vector", nc.vector))}
        final = [sem(f"final{b}") for b in range(2)]
        lead_a = 6
        POOL_CONSTS = 27

        def settled(eng, sem, count):
            wait(eng, sem, count)
            if not isinstance(count, int):
                eng.sem_inc(passed[eng.engine], 1)

        block = ctx.enter_context(nc.Block())

        @block.sync
        def _(sp):
            sp.dma_start(xall[:, 0:lead_a, :], x_tiles[:, 0:lead_a, :]).then_inc(S["x_first"], 16)
            sp.dma_start(wq_in, Wq.rearrange("(k p) c -> p k c", p=P)).then_inc(S["w_in"], 16)
            sp.dma_start(wv_in, Wv.rearrange("(k p) c -> p k c", p=P)).then_inc(S["w_in"], 16)
            for wc, w in ((wqc, q_norm_w), (wvc, v_norm_w)):
                for g in range(KC):
                    sp.dma_start(wc[:, g:g + 1], w[g * HG:(g + 1) * HG, :].rearrange("h e -> (h e)").unsqueeze(1)
                                 ).then_inc(S["wc_in"], 16)
            sp.dma_start(wg[:], Wg.rearrange("(k p) e -> p k e", p=P)).then_inc(S["wg_in"], 16)
            sp.dma_start(xall[:, lead_a:NT, :], x_tiles[:, lead_a:NT, :]).then_inc(S["x_rest"], 16)
            sp.wait_ge(S["consts_pool"], 1)
            sp.dma_start(lists.rearrange("(p b) o -> p (b o)", p=P), pad).then_inc(S["lists_padded"], 16)
            for n, w in enumerate((Ws1, Ws3)):
                sp.dma_start(ws13[:, :, n, :], w.rearrange("(k p) f -> p k f", p=P)).then_inc(S["ws_in"], 16)
            sp.dma_start(ws2[:], Ws2.rearrange("(k p) c -> p k c", p=P)).then_inc(S["ws_in"], 16)
            for n, w in enumerate((W1, W3)):
                for k in range(KC):
                    sp.dma_start(w13[:, :, k, n, :], w[:, k * P:(k + 1) * P, :].rearrange("e p f -> p e f")
                                 ).then_inc(S["w13_in"], 16)

            def step(tile_of):
                if (a := tile_of(2)) is not None:
                    wait(sp, S["xn2_done"], a.t + 1)
                    sp.dma_start(xn2_rows.rearrange("(t p) c -> t p c", p=P)[bass.ds(a.t, 1)].rearrange("a p c -> (a p) c"),
                                 xn2[:, a.b, :]).then_inc(stored[a.b], 16)
            pipelined(sp, NT, 2, lead_a, 4, step)
            sp.wait_ge(S["o_ps"], NT)
            sp.wait_ge(S["ot_ps"], NT)
            sp.wait_ge(S["logits_ps"], NT)
            sp.wait_ge(S["x2T_kept"], NT)
            for b in range(2):
                sp.wait_ge(stored[b], 16 * NT // 2)
            sp.dma_start(w2[:], W2.rearrange("e p c -> p e c")).then_inc(S["w2_in"], 16)

            for b in range(4):
                sp.wait_ge(put[b], 16 * NJ // 4)
            sp.wait_ge(S["z_ps"], NT)
            def rows_step(tile_of):
                if (a := tile_of(0)) is not None:
                    wait(sp, summed, a.t - 1)
                    sp.dma_start(rows[:, a.b], pair_rows.rearrange("(t p k) c -> t p k c", p=P, k=TOP_K)[
                        bass.ds(a.t, 1)].rearrange("a p k c -> (a p) k c")).then_inc(rows_in[a.b], 16)
                if (a := tile_of(2)) is not None:
                    wait(sp, summed, a.t + 1)
                    sp.dma_start(out_tiles[bass.ds(a.t, 1)].rearrange("a p c -> (a p) c"),
                                 xall[:, bass.ds(a.t, 1), :].rearrange("p a c -> p (a c)")).then_inc(final[a.b], 16)
            pipelined(sp, NT, 2, 4, 2, rows_step)
            for b in range(2):
                sp.wait_ge(final[b], 16 * NT // 2)

        @block.gpsimd
        def _(pool):
            def pool_wait(sem, count, most=None):
                settled(pool, sem, count)

            pool.memset(pad, float(PAIRS)).then_inc(S["consts_pool"], 1)
            c = [1]

            def chain(ins):
                c[0] += 1
                ins.then_inc(S["consts_pool"], 1)
                pool.wait_ge(S["consts_pool"], c[0])

            chain(pool.memset(ident[:], 0.0))
            chain(pool.affine_select(out=ident[:], in_=ident[:], compare_op=ALU.not_equal, fill=1.0, base=0,
                                     pattern=[[-1, P]], channel_multiplier=1))
            chain(pool.memset(tri[:], 1.0))
            chain(pool.affine_select(out=tri[:], in_=tri[:], compare_op=ALU.is_ge, fill=0.0, base=0,
                                     pattern=[[1, P]], channel_multiplier=-1))
            chain(pool.memset(tri_bf[:], 1.0))
            chain(pool.affine_select(out=tri_bf[:], in_=tri_bf[:], compare_op=ALU.is_ge, fill=0.0, base=-1,
                                     pattern=[[1, P]], channel_multiplier=-1))
            chain(pool.memset(ones_bf[:], 1.0))
            chain(pool.memset(ones_f[:], 1.0))
            chain(pool.memset(head_mask[:], 1.0))
            for base, mult in ((0, 1), (d - 1, -1)):
                for g in range(KC):
                    v = head_mask[:, g, :].rearrange("p (h e) -> p h e", e=d)
                    chain(pool.affine_select(out=v, in_=v, compare_op=ALU.is_ge, fill=0.0, base=base,
                                             pattern=[[-d * mult, HG], [0, d]], channel_multiplier=mult))
            chain(pool.iota(par_i[:], pattern=[[0, 1]], base=0, channel_multiplier=1))
            chain(pool.iota(eidx_i[:], pattern=[[1, E]], base=0, channel_multiplier=0))
            chain(pool.iota(pair_i[:], pattern=[[P * TOP_K, NT], [1, TOP_K]], base=0, channel_multiplier=TOP_K))
            chain(pool.iota(jc_i[:], pattern=[[P, 2]], base=0, channel_multiplier=1))
            chain(pool.memset(keep[:], 1.0))
            for s in range(B):
                chain(pool.memset(keep[:, s * NTB:s * NTB + 1], 0.0))
            chain(pool.memset(w_raw[:], 0.0))
            chain(pool.memset(w_bd[:], 0.0))
            chain(pool.memset(vp, 0.0))
            chain(pool.memset(mcum[:], 0.0))
            chain(pool.memset(minus_half[:], -0.5))
            chain(pool.memset(eps_col[:], RMS_EPS))
            assert c[0] == POOL_CONSTS
            pool.wait_ge(S["consts_dve"], 5)
            pool.wait_ge(S["lists_padded"], 16)

            def scatter(a, k):
                pool.indirect_dma_start(out=lists, out_offset=bass.IndirectOffsetOnAxis(ap=posi[:, a.b, k:k + 1], axis=0),
                                        in_=pid[:, a.b, k:k + 1], in_offset=None).then_inc(scattered[a.b], 16)

            def step(tile_of):
                if (a := tile_of(0)) is not None:
                    pool_wait(S["mean1"], a.t + 1)
                    pool_wait(S["xn_done"], a.t - 1)
                    pool.tensor_scalar(var1[:], mv1[:, a.b, 1:2], LN_EPS, None, ALU.add).then_inc(S["var1_done"], 1)
                    pool_wait(S["var1_done"], a.t + 1)
                    pool.tensor_tensor(rs1[:, a.b:a.b + 1], var1[:], minus_half[:], ALU.pow
                                       ).then_inc(S["rstd1"], 1)
                if (a := tile_of(3)) is not None:
                    pool_wait(S["x2T_done"], a.t + 1)
                    pool.tensor_copy(x2T_all[:].rearrange("p k (t l) -> p k t l", l=P)[:, :, bass.ds(a.t, 1), :].rearrange("p k a l -> p k (a l)"),
                                     x2T[:, a.b]).then_inc(S["x2T_kept"], 1)
                if (a := tile_of(4)) is not None:
                    pool_wait(scattered[a.b], (a.t - a.b) * 32, None)
                    pool.tensor_copy(pid[:, a.b, :], pair_all[:, bass.ds(a.t, 1), :].rearrange("p a k -> p (a k)")
                                     ).then_inc(S["pid_done"], 1)
                    pool_wait(S["pid_done"], a.t + 1)
                    pool_wait(S["pos_done"], a.t + 1)
                    scatter(a, 0)
                    scatter(a, 1)
                if (a := tile_of(2)) is not None:
                    pool_wait(S["mean2"], a.t + 1)
                    pool_wait(S["xn2_done"], a.t - 1)
                    pool.tensor_scalar(var2[:], mv2[:, a.b, 1:2], LN_EPS, None, ALU.add).then_inc(S["var2_done"], 1)
                    pool_wait(S["var2_done"], a.t + 1)
                    pool.tensor_tensor(rs2[:, a.b:a.b + 1], var2[:], minus_half[:], ALU.pow
                                       ).then_inc(S["rstd2"], 1)
                if (a := tile_of(4)) is not None:
                    scatter(a, 2)
                    scatter(a, 3)
                if (a := tile_of(0)) is not None:
                    pool_wait(S["guess_done"], a.t + 1)
                    pool_wait(S["v_done"], a.t - 1)
                    pool.tensor_scalar(msq[:], ss[:, a.b, :], RMS_EPS, None, ALU.add).then_inc(S["msq_done"], 1)
                    pool.tensor_tensor(gg[:], guess[:], guess[:], ALU.mult).then_inc(S["gg_done"], 1)
                    pool_wait(S["msq_done"], a.t + 1)
                    pool_wait(S["gg_done"], a.t + 1)
                    pool.tensor_tensor(mgg[:], msq[:], gg[:], ALU.mult).then_inc(S["mgg_done"], 1)
                    pool_wait(S["mgg_done"], a.t + 1)
                    pool.tensor_scalar(fac[:], mgg[:], -0.5, 1.5, ALU.mult, ALU.add).then_inc(S["fac_done"], 1)
                    pool_wait(S["fac_done"], a.t + 1)
                    pool.tensor_tensor(rr[:, a.b, :], guess[:], fac[:], ALU.mult).then_inc(S["rms_done"], 1)
            pipelined(pool, NT, 2, lead_a, 4, step)

            pool.wait_ge(S["tab_blk"], 1)
            for b in range(2):
                pool.wait_ge(scattered[b], 64 * NT // 2)
            for n, rows_n in enumerate((P, NJ - P)):
                pool.indirect_dma_start(out=lj[0:rows_n, n, :], out_offset=None, in_=lists_blocks,
                                        in_offset=bass.IndirectOffsetOnAxis(ap=blk_i[0:rows_n, n:n + 1], axis=0)
                                        ).then_inc(S["tab_lj_in"], 16)
            pool.wait_ge(S["tab_done"], 1)

            def expert_step(tile_of):
                if (a := tile_of(0)) is not None:
                    pool_wait(gathered[a.ring], (a.t - a.ring) * 4)
                    pool_wait(S["xT_ps"], a.t - 3)
                    pool.tensor_copy(tok_b[:, a.ring:a.ring + 1], tok_i[:, bass.ds(a.t, 1)]).then_inc(S["bcopy"], 1)
                    pool_wait(S["bcopy"], a.t + 1)
                    pool.indirect_dma_start(out=xg[:, a.ring, :], out_offset=None, in_=xn2_rows,
                                            in_offset=bass.IndirectOffsetOnAxis(ap=tok_b[:, a.ring:a.ring + 1], axis=0)
                                            ).then_inc(gathered[a.ring], 16)
                if (a := tile_of(6)) is not None:
                    pool_wait(put[a.ring], (a.t - a.ring) * 4)
                    pool.tensor_copy(slot_b[:, a.ring:a.ring + 1], slot_i[:, bass.ds(a.t, 1)]).then_inc(S["wt_kept"], 1)
                    pool_wait(S["wt_kept"], a.t + 1)
                    pool_wait(S["y_done"], a.t + 1)
                    pool.indirect_dma_start(out=pair_rows,
                                            out_offset=bass.IndirectOffsetOnAxis(ap=slot_b[:, a.ring:a.ring + 1], axis=0),
                                            in_=y[:, a.ring, :], in_offset=None, bounds_check=PAIRS - 1,
                                            oob_is_err=False).then_inc(put[a.ring], 16)
            pipelined(pool, NJ, 4, 12, 8, expert_step)

        @block.scalar
        def _(act):
            for k in range(KC):
                act.wait_ge(S["wt_ps"], k + 1)
                act.copy(wqv[:, k, :], (pT0, pT1)[k][:]).then_inc(S["wt_done"], 1)

            def step(tile_of):
                if (a := tile_of(0)) is not None:
                    wait(act, S["xnT_ps"], a.t + 1)
                    wait(act, S["qv_ps"], a.t - 1)
                    wait(act, S["scores_ps"], 4 * (a.t - 1))
                    act.copy(xnT[:, a.b], pT0[:, 0:D].rearrange("p (g m) -> p g m", g=KC)).then_inc(S["xnT_done"], 1)
                if (a := tile_of(1)) is not None:
                    wait(act, S["qm_done"], a.t + 1)
                    wait(act, S["o_ps"], a.t)
                    act.copy(qT, pT1[:, 0:D].rearrange("p (g m) -> p g m", g=KC)).then_inc(S["qT_done"], 1)
                if (a := tile_of(3)) is not None:
                    wait(act, S["nmx_done"], a.t + 1)
                    wait(act, S["prob_done"], a.t - 1)
                    act.activation(ex[:, a.b, :], lg[:, a.b, :], ACT.Exp, bias=nmx[:, a.b:a.b + 1], scale=1.0,
                                   accum_out=se[:, a.b:a.b + 1]).then_inc(S["exp_done"], 1)
                if (a := tile_of(0)) is not None:
                    wait(act, S["qv_ps"], a.t + 1)
                    wait(act, S["ss_done"], a.t)
                    act.activation(sq, pQV[:], ACT.Square, scale=float(d) ** -0.5).then_inc(S["sq_done"], 1)
                if (a := tile_of(2)) is not None:
                    wait(act, S["x2T_ps"], a.t + 1)
                    wait(act, S["logits_ps"], a.t - 1)
                    wait(act, S["x2T_kept"], a.t - 1)
                    act.copy(x2T[:, a.b], pT0[:, 0:D].rearrange("p (g m) -> p g m", g=KC)).then_inc(S["x2T_done"], 1)
                if (a := tile_of(0)) is not None:
                    wait(act, S["ss_done"], a.t + 1)
                    act.activation(lnm[:], ss[:, a.b, :], ACT.Ln, bias=eps_col[:]).then_inc(S["ln_done"], 1)
                    wait(act, S["ln_done"], a.t + 1)
                    wait(act, S["rms_done"], a.t)
                    act.activation(guess[:], lnm[:], ACT.Exp, scale=-0.5).then_inc(S["guess_done"], 1)
                if (a := tile_of(1)) is not None:
                    wait(act, S["o_ps"], a.t + 1)
                    wait(act, S["ot_ps"], a.t - 1)
                    for g in range(KC):
                        last = act.activation(oT[:, a.b, g, :], pO[:, g * P:(g + 1) * P], ACT.Copy, scale=wvc[:, g:g + 1])
                    last.then_inc(S["oT_done"], 1)
            act.wait_ge(S["wc_in"], 64)
            act.wait_ge(S["consts_pool"], POOL_CONSTS)
            pipelined(act, NT, 2, lead_a, 4, step)

            def shared_step(tile_of):
                if (a := tile_of(0)) is not None:
                    for m in range(FC):
                        wait(act, S["h_ps"], FC * a.t + m + 1)
                        wait(act, S["gsh_done"], FC * (a.t - 1) + m + 1)
                        act.activation(sg[:, m, :], pS[2 * m][:], ACT.Silu).then_inc(S["silu_done"], 1)
            pipelined(act, NG, 2, 2, 1, shared_step)

            def expert_step(tile_of):
                if (a := tile_of(3)) is not None:
                    wait(act, S["xT_ps"], a.t + 1)
                    wait(act, S["hb_ps"], a.t - 1)
                    act.copy(xgT[:, a.b], pT0[:, 0:D].rearrange("p (g m) -> p g m", g=KC)).then_inc(S["xT_done"], 1)
                if (a := tile_of(4)) is not None:
                    wait(act, S["hb_ps"], a.t + 1)
                    wait(act, S["ge_done"], a.t - 1)
                    act.activation(sge[:, a.b, :], pS[a.b][:, 0:F], ACT.Silu).then_inc(S["sge_done"], 1)
                if (a := tile_of(5)) is not None:
                    wait(act, S["y_ps"], a.t + 1)
                    wait(act, put[a.ring], (a.t - a.ring) * 4)
                    act.copy(y[:, a.ring, :], pS[2 + a.b][:, 0:D]).then_inc(S["y_done"], 1)
            pipelined(act, NJ, 4, 12, 8, expert_step)

        @block.tensor
        def _(pe):
            pe.wait_ge(S["w_in"], 32)
            pe.wait_ge(S["consts_pool"], POOL_CONSTS)
            for k in range(KC):
                for n, w in enumerate((wq_in, wv_in)):
                    for o in range(KC):
                        at = n * D + o * P
                        last = pe.transpose((pT0, pT1)[k][:, at:at + P], w[:, o, k * P:(k + 1) * P], ident[:])
                last.then_inc(S["wt_ps"], 1)
            pe.wait_ge(S["wt_done"], KC)
            pe.wait_ge(S["consts_dve"], 5)
            pe.wait_ge(S["wg_in"], 16)

            def step(tile_of):
                if (a := tile_of(1)) is not None:
                    wait(pe, S["qn_done"], a.t + 1)
                    wait(pe, S["lg_done"], a.t - 1)
                    wait_at_ends(pe, S["qT_done"], a.t)
                    for g in range(KC):
                        last = pe.transpose(pT1[:, g * P:(g + 1) * P], qn[:, a.b, g * P:(g + 1) * P], ident[:])
                    last.then_inc(S["qT_ps"], 1)
                if (a := tile_of(0)) is not None:
                    wait(pe, S["xn_done"], a.t + 1)
                    wait(pe, S["x2T_done"], a.t - 2)
                    wait_at_ends(pe, S["xnT_done"], a.t)
                    wait_at_ends(pe, S["raw_done"], a.t - 1)
                    for g in range(KC):
                        last = pe.transpose(pT0[:, g * P:(g + 1) * P], xn[:, a.b, g * P:(g + 1) * P], ident[:])
                    last.then_inc(S["xnT_ps"], 1)
                if (a := tile_of(1)) is not None:
                    wait(pe, S["qm_done"], a.t + 1)
                    wait(pe, S["masked"], 4 * a.t)
                    for g in range(KC):
                        for j in range(4):
                            last = pe.matmul(pS[j][:, g * 256:(g + 1) * 256], xnT[32 * j:32 * j + 32, a.b, g, :],
                                             qm[32 * j:32 * j + 32, :, g, :], start=(g == 0), stop=True,
                                             skip_group_check=True)
                            if g == KC - 1:
                                last.then_inc(S["scores_ps"], 1)
                if (a := tile_of(2)) is not None:
                    wait(pe, S["oT_done"], a.t + 1)
                    wait(pe, S["qT_done"], a.t + 2, NT)
                    wait_at_ends(pe, S["lg_done"], a.t)
                    for g in range(KC):
                        last = pe.transpose(pT1[:, g * P:(g + 1) * P], oT[:, a.b, g, :], ident[:])
                    last.then_inc(S["ot_ps"], 1)
                if (a := tile_of(0)) is not None:
                    wait(pe, S["xnT_done"], a.t + 1)
                    wait(pe, S["v_done"], a.t)
                    for k in range(KC):
                        last = pe.matmul(pQV[:], xnT[:, a.b, k, :], wqv[:, k, :], start=(k == 0), stop=(k == KC - 1))
                    last.then_inc(S["qv_ps"], 1)
                if (a := tile_of(1)) is not None:
                    wait(pe, S["v_done"], a.t + 1)
                    wait(pe, S["xnT_done"], a.t + 2, NT)
                    wait_at_ends(pe, S["x2T_done"], a.t - 1)
                    for g in range(KC):
                        last = pe.matmul(pT0[:, g * P:(g + 1) * P], xn[:, a.b, g * P:(g + 1) * P],
                                         vp[:, a.b, 4 * g:4 * g + 4, 0:3:2, :], start=True, stop=True)
                    last.then_inc(S["state_ps"], 1)
                if (a := tile_of(3)) is not None:
                    wait(pe, S["mask_done"], a.t + 1)
                    wait(pe, S["mcum_done"], a.t)
                    wait(pe, S["x2_done"], a.t + 2, NT)
                    wait_at_ends(pe, S["lg_done"], a.t + 1)
                    pe.matmul(pT1[:, 0:E], tri_bf[:], mask[:, a.b, :], start=True, stop=False)
                    pe.matmul(pT1[:, 0:E], ones_bf[:], mcum[:, a.b, :], start=False, stop=True).then_inc(S["rank_ps"], 1)
                if (a := tile_of(2)) is not None:
                    wait(pe, S["xn2_done"], a.t + 1)
                    wait(pe, S["raw_done"], a.t + 2, NT)
                    wait_at_ends(pe, S["x2T_done"], a.t)
                    for g in range(KC):
                        last = pe.transpose(pT0[:, g * P:(g + 1) * P], xn2[:, a.b, g * P:(g + 1) * P], ident[:])
                    last.then_inc(S["x2T_ps"], 1)
                if (a := tile_of(1)) is not None:
                    wait(pe, S["qT_done"], a.t + 1)
                    wait(pe, S["state_done"], a.t)
                    wait(pe, S["oT_done"], a.t)
                    for g in range(KC):
                        pe.matmul(pO[:, g * P:(g + 1) * P], w_bd[:, a.b, g * P:(g + 1) * P], qT[:, g, :],
                                  start=(g == 0), stop=False, skip_group_check=True)
                    for g in range(KC):
                        for r in range(2):
                            for j in range(4):
                                if g == 0 and r == 0:
                                    wait(pe, S["masked"], 4 * a.t + j + 1)
                                last = pe.matmul(pO[32 * j:32 * j + 32, g * P:(g + 1) * P],
                                                 vp[:, a.b, 4 * g + j, r:r + 2, :], s_sb[:, j, g, r, :],
                                                 start=False, stop=(r == 1), skip_group_check=True)
                    last.then_inc(S["o_ps"], 1)
                if (a := tile_of(2)) is not None:
                    wait(pe, S["x2T_done"], a.t + 1)
                    wait(pe, S["x2_done"], a.t + 1)
                    wait(pe, S["placed_done"], a.t)
                    for k in range(KC):
                        last = pe.matmul(pT1[:, 0:E], x2T[:, a.b, k, :], wg[:, k, :], start=(k == 0), stop=(k == KC - 1))
                    last.then_inc(S["logits_ps"], 1)
            pipelined(pe, NT, 2, lead_a, 4, step)

            pe.wait_ge(S["mcum_done"], NT)
            pe.wait_ge(S["placed_done"], NT)
            pe.wait_ge(S["lg_done"], NT)
            pe.matmul(pT1[:, 0:E], ones_bf[:], mcum[:, NT % 2, :], start=True, stop=True).then_inc(S["cnt_ps"], 1)

            pe.wait_ge(S["ws_in"], 48)
            pe.wait_ge(S["x2T_kept"], NT)
            pe.wait_ge(S["masked"], 4 * NT)

            def shared_step(tile_of):
                if (a := tile_of(0)) is not None:
                    for m in range(FC):
                        wait(pe, S["gsh_done"], FC * (a.t - 1) + m + 1)
                        for n in range(2):
                            for k in range(KC):
                                last = pe.matmul(pS[2 * m + n][:], ws13[:, k, n, m * P:(m + 1) * P],
                                                 x2T_all[:, k, bass.ds(a.t * TG, TG)], start=(k == 0), stop=(k == KC - 1))
                        last.then_inc(S["h_ps"], 1)
                if (a := tile_of(1)) is not None:
                    wait(pe, S["gsh_done"], FC * (a.t + 1))
                    for q in range(TG // P):
                        wait(pe, S["z_done"], 4 * a.t + q - 1)
                        for m in range(FC):
                            last = pe.matmul((pQV, pO)[q % 2][:, 0:D], gsh[:, a.b, m, q * P:(q + 1) * P], ws2[:, m, :],
                                             start=(m == 0), stop=(m == FC - 1))
                        last.then_inc(S["z_ps"], 1)
            pipelined(pe, NG, 2, 4, 1, shared_step)

            pe.wait_ge(S["tab_blk"], 1)
            for n in range(2):
                last = pe.matmul(pT1[0:1, n * P:(n + 1) * P], ejc[:, n:n + 1], ident[:], start=True, stop=True)
            last.then_inc(S["erow_ps"], 1)
            pe.wait_ge(S["tab_lj_in"], 32)
            pe.transpose(pT0[:, 0:P], lj[:, 0, :], ident[:])
            pe.transpose(pT0[:, P:NJ], lj[0:NJ - P, 1, :], ident[0:NJ - P, 0:NJ - P]).then_inc(S["tab_ps"], 1)
            pe.wait_ge(S["tab_done"], 1)
            pe.wait_ge(S["erow_done"], 1)
            pe.wait_ge(S["w13_in"], 16 * 2 * KC)
            pe.wait_ge(S["w2_in"], 16)

            def expert_step(tile_of):
                if (a := tile_of(3)) is not None:
                    wait(pe, gathered[a.ring], (a.t - a.ring) * 4 + 16)
                    wait(pe, S["xT_done"], a.t)
                    for g in range(KC):
                        last = pe.transpose(pT0[:, g * P:(g + 1) * P], xg[:, a.ring, g * P:(g + 1) * P], ident[:])
                    last.then_inc(S["xT_ps"], 1)
                if (a := tile_of(5)) is not None:
                    wait(pe, S["ge_done"], a.t + 1)
                    wait(pe, S["gT_done"], a.t)
                    pe.transpose(pT1[:, 0:P], ge[:, a.b, :], ident[:]).then_inc(S["gT_ps"], 1)
                if (a := tile_of(4)) is not None:
                    e = pe.value_load(erow[0:1, bass.ds(a.t, 1)], min_val=0, max_val=E - 1)
                    wait(pe, S["xT_done"], a.t + 1)
                    wait(pe, S["ge_done"], a.t - 1)
                    for k in range(KC):
                        last = pe.matmul(pS[a.b][:, 0:2 * F], xgT[:, a.b, k, :],
                                         w13[:, bass.ds(e, 1), k, :, :].rearrange("p a n f -> p (a n f)"),
                                         start=(k == 0), stop=(k == KC - 1))
                    last.then_inc(S["hb_ps"], 1)
                if (a := tile_of(5)) is not None:
                    e = pe.value_load(erow[0:1, bass.ds(a.t, 1)], min_val=0, max_val=E - 1)
                    wait(pe, S["gT_done"], a.t + 1)
                    wait(pe, S["y_done"], a.t - 1)
                    pe.matmul(pS[2 + a.b][:, 0:D], geT[:, a.b, :],
                              w2[:, bass.ds(e, 1), :].rearrange("p a c -> p (a c)"), start=True, stop=True
                              ).then_inc(S["y_ps"], 1)
            pipelined(pe, NJ, 4, 12, 8, expert_step)

        @block.vector
        def _(dve):
            dve.wait_ge(S["consts_pool"], POOL_CONSTS)
            dve.wait_ge(S["wc_in"], 64)
            c = [0]

            def chain(ins):
                c[0] += 1
                ins.then_inc(S["consts_dve"], 1)
                dve.wait_ge(S["consts_dve"], c[0])

            chain(dve.tensor_scalar(par_i[:], par_i[:], 4, 1, ALU.logical_shift_right, ALU.bitwise_and))
            chain(dve.tensor_copy(par_f[:, 1:2], par_i[:]))
            chain(dve.tensor_scalar(par_f[:, 0:1], par_f[:, 1:2], -1.0, 1.0, ALU.mult, ALU.add))
            chain(dve.tensor_copy(eidx[:], eidx_i[:]))
            chain(dve.tensor_copy(pair_all[:].rearrange("p t k -> p (t k)"), pair_i[:]))
            chain(dve.tensor_scalar(ebase[:], eidx[:], float(T), None, ALU.mult))
            for r in range(2):
                chain(dve.tensor_scalar(mwq[:, r, :], wqc[:], par_f[:, r:r + 1], None, ALU.mult))
            for g in range(KC):
                chain(dve.tensor_scalar(head_mask[:, g, :], head_mask[:, g, :], wqc[:, g:g + 1], None, ALU.mult))
            chain(dve.tensor_copy(jc[:], jc_i[:]))

            def stats(src, buf, dst, done, mean, t):
                dve.bn_stats(buf[:], src).then_inc(S[done], 1)
                settled(dve, S[done], t + 1)
                dve.bn_aggr(dst, buf[:]).then_inc(S[mean], 1)

            def x_tile(a):
                return xall[:, bass.ds(a.t, 1), :].rearrange("p a c -> p (a c)")

            def masked(a, j):
                wait(dve, S["scores_ps"], 4 * a.t + j + 1)
                wait(dve, S["o_ps"], a.t)
                dve.tensor_tensor(s_sb[:, j].rearrange("p g r l -> p (g r) l"), pS[j][:].rearrange("p (n l) -> p n l", l=P),
                                  tri[:].unsqueeze(1).to_broadcast([P, 4, P]), ALU.mult).then_inc(S["masked"], 1)

            def step(tile_of):
                a0, a1, a2, a3 = (tile_of(s) for s in range(4))
                if a0 is not None:
                    stats(x_tile(a0), st, mv1[:, a0.b, :], "stats1", "mean1", a0.t)
                if a3 is not None:
                    wait(dve, S["logits_ps"], a3.t + 1)
                    wait(dve, S["exp_done"], a3.t - 1)
                    dve.tensor_copy(lg[:, a3.b, :], pT1[:, 0:E]).then_inc(S["lg_done"], 1)
                    settled(dve, S["lg_done"], a3.t + 1)
                    dve.max(m8[:], lg[:, a3.b, :]).then_inc(S["max_done"], 1)
                    wait(dve, S["max_done"], a3.t + 1)
                    dve.tensor_scalar(nmx[:, a3.b:a3.b + 1], m8[:, 0:1], -1.0, None, ALU.mult).then_inc(S["nmx_done"], 1)
                if a1 is not None:
                    wait(dve, S["qT_ps"], a1.t + 1)
                    wait(dve, S["scores_ps"], 4 * a1.t)
                    dve.tensor_tensor(qm, pT1[:, 0:D].rearrange("p (g l) -> p g l", g=KC).unsqueeze(1).to_broadcast([P, 2, KC, P]),
                                      mwq[:].unsqueeze(3).to_broadcast([P, 2, KC, P]), ALU.mult).then_inc(S["qm_done"], 1)
                if a0 is not None:
                    wait(dve, S["rstd1"], a0.t + 1)
                    wait(dve, S["state_ps"], a0.t - 1)
                    dve.tensor_scalar(xn[:, a0.b, :], x_tile(a0), mv1[:, a0.b, 0:1], rs1[:, a0.b:a0.b + 1],
                                      ALU.subtract, ALU.mult).then_inc(S["xn_done"], 1)
                if a1 is not None:
                    masked(a1, 0)
                if a2 is not None:
                    wait(dve, S["ot_ps"], a2.t + 1)
                    dve.tensor_tensor(x_tile(a2), x_tile(a2), pT1[:, 0:D], ALU.add).then_inc(S["x2_done"], 1)
                    settled(dve, S["x2_done"], a2.t + 1)
                    stats(x_tile(a2), st2, mv2[:, a2.b, :], "stats2", "mean2", a2.t)
                if a1 is not None:
                    masked(a1, 1)
                if a3 is not None:
                    t1 = a3.t + 1
                    wait(dve, S["exp_done"], t1)
                    dve.reciprocal(rin[:], se[:, a3.b:a3.b + 1]).then_inc(S["rin_done"], 1)
                    wait(dve, S["rin_done"], t1)
                    dve.tensor_scalar(prob[:], ex[:, a3.b, :], rin[:], None, ALU.mult).then_inc(S["prob_done"], 1)
                    settled(dve, S["prob_done"], t1)
                    dve.max(t8[:], prob[:]).then_inc(S["top_done"], 1)
                    settled(dve, S["top_done"], t1)
                    dve.max_index(ix[:], t8[:], prob[:]).then_inc(S["ix_done"], 1)
                    dve.tensor_copy(wts[:, bass.ds(a3.t, 1), :].rearrange("p a k -> p (a k)"), t8[:, 0:TOP_K])
                    wait(dve, S["ix_done"], t1)
                    dve.tensor_copy(ixf[:], ix[:, 0:TOP_K]).then_inc(S["ixf_done"], 1)
                    wait(dve, S["ixf_done"], t1)
                    dve.tensor_tensor(oh[:], eidx[:].unsqueeze(1).to_broadcast([P, TOP_K, E]),
                                      ixf[:].unsqueeze(2).to_broadcast([P, TOP_K, E]), ALU.is_equal).then_inc(S["oh_done"], 1)
                    wait(dve, S["oh_done"], t1)
                    with nc.allow_low_precision("0 and 1 are exact"):
                        dve.tensor_reduce(mask[:, a3.b, :], oh[:].rearrange("p k e -> p e k"), AX_X, ALU.add
                                          ).then_inc(S["mask_done"], 1)
                    wait(dve, S["mask_done"], t1)
                    wait(dve, S["rank_ps"], a3.t)
                    dve.tensor_tensor(mcum[:, 1 - a3.b, :], mcum[:, a3.b, :], mask[:, a3.b, :], ALU.add
                                      ).then_inc(S["mcum_done"], 1)
                if a1 is not None:
                    t1 = a1.t + 1
                    wait(dve, S["state_ps"], t1)
                    dve.scalar_tensor_tensor(out=w_raw[:], in0=w_raw[:], scalar=keep[:, bass.ds(a1.t, 1)], in1=pT0[:, 0:D],
                                             op0=ALU.mult, op1=ALU.add).then_inc(S["raw_done"], 1)
                    wait(dve, S["raw_done"], t1)
                    wait(dve, S["o_ps"], a1.t)
                    dve.scalar_tensor_tensor(out=w_bd[:, 1 - a1.b, :], in0=w_raw[:], scalar=keep[:, bass.ds(a1.t + 1, 1)],
                                             in1=head_mask[:].rearrange("p g c -> p (g c)"), op0=ALU.mult, op1=ALU.mult
                                             ).then_inc(S["state_done"], 1)
                if a2 is not None:
                    wait(dve, S["rstd2"], a2.t + 1)
                    wait(dve, S["x2T_ps"], a2.t - 1)
                    wait(dve, stored[a2.b], (a2.t - a2.b) * 8)
                    dve.tensor_scalar(xn2[:, a2.b, :], x_tile(a2), mv2[:, a2.b, 0:1], rs2[:, a2.b:a2.b + 1],
                                      ALU.subtract, ALU.mult).then_inc(S["xn2_done"], 1)
                if a1 is not None:
                    masked(a1, 2)
                if a0 is not None:
                    wait(dve, S["sq_done"], a0.t + 1)
                    wait(dve, S["rms_done"], a0.t - 1)
                    dve.tensor_reduce(ss[:, a0.b, :], sq.rearrange("p (h e) -> p h e", e=d), AX_X, ALU.add
                                      ).then_inc(S["ss_done"], 1)
                if a1 is not None:
                    masked(a1, 3)
                if a3 is not None:
                    t1 = a3.t + 1
                    wait(dve, S["rank_ps"], t1)
                    dve.tensor_tensor(place[:], pT1[:, 0:E], ebase[:], ALU.add).then_inc(S["placed_done"], 1)
                    wait(dve, S["placed_done"], t1)
                    dve.tensor_tensor(ohr[:], oh[:], place[:].unsqueeze(1).to_broadcast([P, TOP_K, E]), ALU.mult
                                      ).then_inc(S["place_done"], 1)
                    wait(dve, S["place_done"], t1)
                    dve.tensor_reduce(pos[:], ohr[:], AX_X, ALU.add).then_inc(S["pos_kept"], 1)
                    wait(dve, S["pos_kept"], t1)
                    wait(dve, scattered[a3.b], (a3.t - a3.b) * 32)
                    dve.tensor_copy(posi_all[:, bass.ds(a3.t, 1), :].rearrange("p a k -> p (a k)"), pos[:])
                    dve.tensor_copy(posi[:, a3.b, :], pos[:]).then_inc(S["pos_done"], 1)
                if a0 is not None:
                    wait(dve, S["rms_done"], a0.t + 1)
                    wait(dve, S["qT_ps"], a0.t - 1)
                    dve.tensor_tensor(qn[:, a0.b, :].rearrange("p (h e) -> p h e", e=d), pQV[:, 0:D].rearrange("p (h e) -> p h e", e=d),
                                      rr[:, a0.b, 0:H].unsqueeze(2).to_broadcast([P, H, d]), ALU.mult).then_inc(S["qn_done"], 1)
                    wait(dve, S["o_ps"], a0.t - 1)
                    dve.tensor_tensor(vp[:, a0.b, :, 0:3:2, :], pQV[:, D:2 * D].rearrange("p (n r e) -> p n r e", r=2, e=d),
                                      rr[:, a0.b, H:2 * H].rearrange("p (n r) -> p n r", r=2).unsqueeze(3).to_broadcast([P, NP_, 2, d]),
                                      ALU.mult).then_inc(S["v_done"], 1)

            dve.wait_ge(S["x_first"], 16)

            dve.wait_ge(S["x_rest"], 16)
            pipelined(dve, NT, 2, lead_a, 4, step)

            r = [0]

            def tab(ins, done="tabs"):
                r[0] += 1
                ins.then_inc(S["tabs"], 1)
                dve.wait_ge(S["tabs"], r[0])

            dve.wait_ge(S["cnt_ps"], 1)
            tab(dve.tensor_scalar(cnt_i[:], pT1[:, 0:E], float(P - 1), None, ALU.add))
            tab(dve.tensor_scalar(nt_i[:], cnt_i[:], 7, None, ALU.logical_shift_right))
            tab(dve.tensor_copy(ntf[:], nt_i[:]))
            tab(dve.tensor_tensor_scan(endt[:], ones_f[:], ntf[:], 0.0, ALU.mult, ALU.add))
            for n in range(2):
                tab(dve.tensor_scalar(behind[:, n, :], endt[:], jc[:, n:n + 1], None, ALU.is_le))
            tab(dve.tensor_reduce(ej[:], behind[:], AX_X, ALU.add))
            tab(dve.tensor_tensor(bnt[:], behind[:], ntf[:].unsqueeze(1).to_broadcast([P, 2, E]), ALU.mult))
            tab(dve.tensor_reduce(stj[:], bnt[:], AX_X, ALU.add))
            tab(dve.tensor_tensor(jrel[:], jc[:], stj[:], ALU.subtract))
            tab(dve.scalar_tensor_tensor(out=blk[:], in0=ej[:], scalar=float(NBE), in1=jrel[:], op0=ALU.mult, op1=ALU.add))
            tab(dve.tensor_scalar(blk_i[:], blk[:], float(NB), None, ALU.min))
            tab(dve.tensor_scalar(ejc[:], ej[:], float(E - 1), None, ALU.min))
            dve.tensor_copy(jrel[:], jc[:]).then_inc(S["tab_blk"], 1)
            flat_w = wts[:].rearrange("p t k -> p (t k)")
            tab(dve.tensor_scalar(rank_i[:], posi_all[:].rearrange("p t k -> p (t k)"), T - 1, None, ALU.bitwise_and))
            tab(dve.tensor_scalar(inside[:], rank_i[:], float(CAP), None, ALU.is_lt))
            tab(dve.tensor_tensor(flat_w, flat_w, inside[:], ALU.mult))

            def shared_step(tile_of):
                if (a := tile_of(0)) is not None:
                    for m in range(FC):
                        wait(dve, S["silu_done"], FC * a.t + m + 1)
                        wait(dve, S["z_ps"], 4 * (a.t - 1))
                        dve.tensor_tensor(gsh[:, a.b, m, :], sg[:, m, :], pS[2 * m + 1][:], ALU.mult).then_inc(S["gsh_done"], 1)
                if (a := tile_of(1)) is not None:
                    for q in range(TG // P):
                        wait(dve, S["z_ps"], 4 * a.t + q + 1)
                        xt = xall[:, bass.ds(a.t * (TG // P) + q, 1), :].rearrange("p a c -> p (a c)")
                        dve.tensor_tensor(xt, xt, (pQV, pO)[q % 2][:, 0:D], ALU.add).then_inc(S["z_done"], 1)
            dve.wait_ge(S["lists_padded"], 16)
            pipelined(dve, NG, 2, 4, 1, shared_step)

            dve.wait_ge(S["erow_ps"], 1)
            dve.tensor_copy(erow[:], pT1[0:1, 0:256]).then_inc(S["erow_done"], 1)
            dve.wait_ge(S["tab_ps"], 1)
            tab(dve.tensor_copy(slot_i[:], pT0[:, 0:NJ]))
            tab(dve.tensor_scalar(tok_i[:], slot_i[:], 2, None, ALU.logical_shift_right))
            dve.tensor_scalar(tok_i[:], tok_i[:], float(T - 1), None, ALU.min).then_inc(S["tab_done"], 1)

            def expert_step(tile_of):
                if (a := tile_of(5)) is not None:
                    wait(dve, S["gT_ps"], a.t + 1)
                    wait(dve, S["y_ps"], a.t - 1)
                    dve.tensor_copy(geT[:, a.b, :], pT1[:, 0:P]).then_inc(S["gT_done"], 1)
                if (a := tile_of(4)) is not None:
                    wait(dve, S["sge_done"], a.t + 1)
                    wait(dve, S["gT_ps"], a.t - 1)
                    dve.tensor_tensor(ge[:, a.b, :], sge[:, a.b, :], pS[a.b][:, F:2 * F], ALU.mult).then_inc(S["ge_done"], 1)
            pipelined(dve, NJ, 4, 12, 8, expert_step)

            def sum_step(tile_of):
                if (a := tile_of(0)) is not None:
                    wait(dve, rows_in[a.b], (a.t - a.b) * 8 + 16)
                    for k in range(TOP_K):
                        ins = dve.scalar_tensor_tensor(out=x_tile(a), in0=rows[:, a.b, k, :],
                                                       scalar=wts[:, bass.ds(a.t, 1), k:k + 1].rearrange("p a k -> p (a k)"),
                                                       in1=x_tile(a), op0=ALU.mult, op1=ALU.add)
                        if k < TOP_K - 1:
                            ins.then_inc(S["ridx_ps"], 1)
                            wait(dve, S["ridx_ps"], (TOP_K - 1) * a.t + k + 1)
                        else:
                            ins.then_inc(summed, 1)
            pipelined(dve, NT, 2, 4, 1, sum_step)


_INS = ["L0_attn_X", "L0_attn_Wq", "L0_attn_Wv", "L0_attn_q_norm_w", "L0_attn_v_norm_w", "L0_ffn_Wg", "L0_ffn_W1",
        "L0_ffn_W2", "L0_ffn_W3", "L0_ffn_Ws1", "L0_ffn_Ws2", "L0_ffn_Ws3"]


def kernel(**inputs):
    import numpy as _np
    import concourse.bacc as _bacc
    from concourse import mybir as _mybir
    from concourse.bass_utils import run_bass_kernel_spmd as _run

    nc = _bacc.Bacc("TRN2", target_bir_lowering=False, num_devices=1)
    arrays, args = {}, []
    for name in _INS:
        a = _np.ascontiguousarray(inputs[name])
        arrays[f"in_{name}"] = a
        args.append(nc.dram_tensor(f"in_{name}", a.shape, _mybir.dt.from_np(a.dtype), kind="ExternalInput").ap())
    shape = inputs["L0_attn_X"].shape
    args.append(nc.dram_tensor("out", shape, _mybir.dt.float32, kind="ExternalOutput").ap())
    build(nc, *args)
    r = _run(nc, [arrays], core_ids=[0])
    return r.results[0]["out"]
```

```python
from contextlib import ExitStack

import concourse.bass as bass
from concourse import mybir

F32 = mybir.dt.float32
BF16 = mybir.dt.bfloat16
I32 = mybir.dt.int32
U32 = mybir.dt.uint32
ALU = mybir.AluOpType
ACT = mybir.ActivationFunctionType
AX_X = mybir.AxisListType.X

P = 128
LN_EPS = 1e-5
RMS_EPS = 1e-8
TOP_K = 4
CAP_FACTOR = 4


class Tile:

    def __init__(self, t, ring, turn=None):
        self.t, self.ring = t, ring
        self.b = ring % 2
        self.turn = turn


def pipelined(eng, n, unroll, lead, depth, step, before_loop=None):
    def peeled(i):
        def tile_of(skew):
            return Tile(i - skew, (i - skew) % 4, i // unroll) if 0 <= i - skew < n else None
        step(tile_of)

    def looped(r, k):
        def tile_of(skew):
            return Tile(r * unroll + (k - skew), (k - skew) % unroll if unroll == 4 else (k - skew) % 2, r)
        step(tile_of)

    assert lead % unroll == 0 and n % unroll == 0
    for i in range(lead):
        peeled(i)
    if before_loop is not None:
        before_loop()
    with eng.Fori(lead // unroll, n // unroll) as r:
        for k in range(unroll):
            looped(r, k)
    for i in range(n, n + depth):
        peeled(i)


def wait(eng, sem, count, most=None):
    if isinstance(count, int):
        if count <= 0:
            return
        if most is not None:
            count = min(count, most)
    eng.wait_ge(sem, count)


def wait_at_ends(eng, sem, count, most=None):
    if isinstance(count, int):
        wait(eng, sem, count, most)


def build(nc, X, Wq, Wv, q_norm_w, v_norm_w, Wg, W1, W2, W3, Ws1, Ws2, Ws3, out):
    B, L, D = X.shape
    H, d = q_norm_w.shape
    E = Wg.shape[1]
    F = W1.shape[2]
    FS = Ws1.shape[1]
    T = B * L
    NT = T // P
    NTB = L // P
    KC = D // P
    FC = FS // P
    PAIRS = T * TOP_K
    CAP = CAP_FACTOR * PAIRS // E
    NBE = T // P
    NB = E * NBE
    NJ = PAIRS // P + E
    HG = P // d
    NP_ = H // 2
    TG = 512
    NG = T // TG
    assert D == 256 and d == 16 and F == 128 and FS == 256 and E == 32

    ctx = ExitStack()
    with ctx:
        def sb(name, shape, dt=F32):
            return ctx.enter_context(nc.sbuf_tensor(name, shape, dt))

        def pb(name):
            return ctx.enter_context(nc.psum_tensor(name, [P, 512], F32))

        def sem(name):
            return ctx.enter_context(nc.semaphore(name))

        xn2_rows = nc.dram_tensor("xn2_rows", [T, D], F32).ap()
        lists = nc.dram_tensor("lists", [(NB + 1) * P, 1], F32).ap()
        y_rows = nc.dram_tensor("y_rows", [NJ * P, D], F32).ap()
        lists_blocks = lists.rearrange("(b r) o -> b (r o)", r=P)

        x_tiles = X.rearrange("b (t p) c -> p (b t) c", p=P)
        out_tiles = out.rearrange("b (t p) c -> (b t) p c", p=P)

        xall = sb("xall", [P, NT, D])
        x2T_all = sb("x2T_all", [P, KC, T])
        w13 = sb("w13", [P, E, KC, 2, F])
        w2 = sb("w2", [P, E, D])
        ws13 = sb("ws13", [P, KC, 2, FS])
        ws2 = sb("ws2", [P, FC, D])
        ident = sb("ident", [P, P])
        tri = sb("tri", [P, P])
        keep = sb("keep", [P, NT + 2])
        wqc = sb("wqc", [P, KC])
        wvc = sb("wvc", [P, KC])
        wg = sb("wg", [P, KC, E])
        par_i = sb("par_i", [P, 1], I32)
        par_f = sb("par_f", [P, 2])
        mwq = sb("mwq", [P, 2, KC])
        head_mask = sb("head_mask", [P, KC, P])
        tri_bf = sb("tri_bf", [P, P], BF16)
        ones_bf = sb("ones_bf", [P, P], BF16)
        eidx_i = sb("eidx_i", [P, NJ // 4], I32)
        eidx = sb("eidx", [P, NJ // 4])
        ebase = sb("ebase", [P, E])
        pair_i = sb("pair_i", [P, NT * TOP_K], I32)
        pair_all = sb("pair_all", [P, NT, TOP_K])

        st = sb("st", [P, 6])
        mv1 = sb("mv1", [P, 2, 2])
        rs1 = sb("rs1", [P, 2])
        st2 = sb("st2", [P, 6])
        mv2 = sb("mv2", [P, 2, 2])
        rs2 = sb("rs2", [P, 2])
        ss = sb("ss", [P, 2, 2 * H])
        rr = sb("rr", [P, 2, 2 * H])
        var1 = sb("var1", [P, 1])
        var2 = sb("var2", [P, 1])
        minus_half = sb("minus_half", [P, 1])
        eps_col = sb("eps_col", [P, 1])
        lnm = sb("lnm", [P, 2 * H])
        guess = sb("guess", [P, 2 * H])
        msq = sb("msq", [P, 2 * H])
        gg = sb("gg", [P, 2 * H])
        mgg = sb("mgg", [P, 2 * H])
        fac = sb("fac", [P, 2 * H])
        w_raw = sb("w_raw", [P, KC * P])
        w_bd = sb("w_bd", [P, 2, KC * P])
        lg = sb("lg", [P, 2, E])
        m8 = sb("m8", [P, 8])
        nmx = sb("nmx", [P, 2])
        ex = sb("ex", [P, 2, E])
        se = sb("se", [P, 2])
        rin = sb("rin", [P, 1])
        prob = sb("prob", [P, E])
        t8 = sb("t8", [P, 8])
        ix = sb("ix", [P, 8], U32)
        ixf = sb("ixf", [P, TOP_K])
        oh = sb("oh", [P, TOP_K, E])
        ohr = sb("ohr", [P, TOP_K, E])
        mask = sb("mask", [P, 2, E], BF16)
        mcum = sb("mcum", [P, 2, E], BF16)
        rk = sb("rk", [P, E])
        place = sb("place", [P, E])
        pos = sb("pos", [P, TOP_K])
        posi = sb("posi", [P, 2, TOP_K], I32)
        pid = sb("pid", [P, 2, TOP_K])
        posi_all = sb("posi_all", [P, NT, TOP_K], I32)
        wts = sb("wts", [P, NT, TOP_K])

        arena = w2[:].rearrange("p e c -> p (e c)")
        cut = [0]

        def part(width):
            cut[0] += width
            assert cut[0] <= E * D
            return arena[:, cut[0] - width:cut[0]]

        s_sb = part(2048).rearrange("p (j g r l) -> p j g r l", j=4, g=2, r=2)
        sq = part(512)
        qm = part(512).rearrange("p (r g l) -> p r g l", r=2, g=2)
        qn = part(512).rearrange("p (b c) -> p b c", b=2)
        qT = part(256).rearrange("p (g l) -> p g l", g=2)
        vp = part(2 * NP_ * 3 * d).rearrange("p (b n k e) -> p b n k e", b=2, n=NP_, k=3)
        xn = part(512).rearrange("p (b c) -> p b c", b=2)
        xnT = part(512).rearrange("p (b g m) -> p b g m", b=2, g=2)
        oT = part(512).rearrange("p (b g l) -> p b g l", b=2, g=2)
        xn2 = part(512).rearrange("p (b c) -> p b c", b=2)
        x2T = part(512).rearrange("p (b g l) -> p b g l", b=2, g=2)
        wqv = part(KC * 512).rearrange("p (k c) -> p k c", k=KC)
        A_END = cut[0]
        wq_in = s_sb.rearrange("p j g r l -> p (j g r l)")[:, 0:512].rearrange("p (k c) -> p k c", k=2)
        wv_in = s_sb.rearrange("p j g r l -> p (j g r l)")[:, 512:1024].rearrange("p (k c) -> p k c", k=2)

        sg = sb("sg", [P, FC, TG])
        gsh = sb("gsh", [P, 2, FC, TG])
        pad = gsh[:].rearrange("p b f t -> p (b f t)")[:, 0:NB + 1]
        xg = sb("xg", [P, 4, D])
        after_a = gsh[:].rearrange("p b f t -> p (b f t)")
        xgT = after_a[:, 0:512].rearrange("p (b g m) -> p b g m", b=2, g=KC)
        sge = after_a[:, 512:768].rearrange("p (b f) -> p b f", b=2)
        ge = after_a[:, 768:1024].rearrange("p (b f) -> p b f", b=2)
        geT = after_a[:, 1024:1280].rearrange("p (b f) -> p b f", b=2)
        y = sg[:].rearrange("p f t -> p (f t)").rearrange("p (b c) -> p b c", b=4)
        rows = w13[:, 0:8].rearrange("p e k n f -> p (e k n f)").rearrange("p (b k c) -> p b k c", b=4, k=TOP_K)
        place_e = sb("place_e", [P, NT * TOP_K], I32)
        place_ef = sb("place_ef", [P, NT * TOP_K])
        shift = sb("shift", [P, NJ // 4])
        moved = sb("moved", [P, NT * TOP_K])
        rowf = sb("rowf", [P, NT * TOP_K])
        row_i = sb("row_i", [P, NT, TOP_K], I32)
        row_b = sb("row_b", [P, 4, TOP_K], I32)
        cnt_i = sb("cnt_i", [P, E], I32)
        nt_i = sb("nt_i", [P, E], I32)
        ntf = sb("ntf", [P, E])
        ones_f = sb("ones_f", [P, E])
        endt = sb("endt", [P, E])
        jc_i = sb("jc_i", [P, 2], I32)
        jc = sb("jc", [P, 2])
        behind = sb("behind", [P, 2, E])
        ej = sb("ej", [P, 2])
        bnt = sb("bnt", [P, 2, E])
        stj = sb("stj", [P, 2])
        jrel = sb("jrel", [P, 2])
        blk = sb("blk", [P, 2])
        blk_i = sb("blk_i", [P, 2], I32)
        ejc = sb("ejc", [P, 2])
        erow = sb("erow", [1, 256], I32)
        lj = sb("lj", [P, 2, P])
        slot_i = sb("slot_i", [P, NJ], I32)
        tok_i = sb("tok_i", [P, NJ], I32)
        tok_b = sb("tok_b", [P, 4], I32)
        rank_i = sb("rank_i", [P, NT * TOP_K], I32)
        inside = sb("inside", [P, NT * TOP_K])

        pT0, pT1, pQV, pO = pb("pT0"), pb("pT1"), pb("pQV"), pb("pO")
        pS = [pb(f"pS{j}") for j in range(4)]

        names = """var1_done var2_done ln_done guess_done msq_done gg_done mgg_done fac_done x_first x_rest w_in wc_in wg_in consts_pool consts_dve wt_ps wt_done
            stats1 mean1 rstd1 xn_done xnT_ps xnT_done qv_ps sq_done ss_done rms_done qn_done v_done
            qT_ps qm_done qT_done scores_ps masked state_ps raw_done state_done o_ps oT_done
            ot_ps x2_done stats2 mean2 rstd2 xn2_done x2T_ps x2T_done logits_ps
            lg_done max_done nmx_done exp_done rin_done prob_done top_done ix_done ixf_done oh_done mask_done
            mcum_done rank_ps place_done placed_done pos_done pos_kept pid_done lists_padded
            w13_in w2_in ws_in h_ps silu_done gsh_done z_ps z_done
            cnt_ps tabs tab_blk tab_lj_in tab_ps tab_done erow_ps erow_done added
            bcopy xT_ps xT_done hb_ps sge_done ge_done gT_ps gT_done y_ps y_done row_tab row_done rcopy summed moved_done s_copied masked_pool rk_done""".split()
        S = {n: sem(n) for n in names}
        stored = [sem(f"stored{b}") for b in range(2)]
        scattered = [sem(f"scattered{b}") for b in range(2)]
        gathered = [sem(f"gathered{b}") for b in range(4)]
        put = [sem(f"put{b}") for b in range(4)]
        rows_in = [sem(f"rows_in{b}") for b in range(4)]
        passed = {e.engine: sem(n) for n, e in (("passed_pool", nc.gpsimd), ("passed_vector", nc.vector))}
        final = [sem(f"final{b}") for b in range(2)]
        lead_a = 8
        POOL_CONSTS = 27

        def settled(eng, sem, count):
            wait(eng, sem, count)
            if not isinstance(count, int):
                eng.sem_inc(passed[eng.engine], 1)

        block = ctx.enter_context(nc.Block())

        @block.sync
        def _(sp):
            sp.dma_start(xall[:, 0:lead_a, :], x_tiles[:, 0:lead_a, :]).then_inc(S["x_first"], 16)
            sp.dma_start(wq_in, Wq.rearrange("(k p) c -> p k c", p=P)).then_inc(S["w_in"], 16)
            sp.dma_start(wv_in, Wv.rearrange("(k p) c -> p k c", p=P)).then_inc(S["w_in"], 16)
            for wc, w in ((wqc, q_norm_w), (wvc, v_norm_w)):
                for g in range(KC):
                    sp.dma_start(wc[:, g:g + 1], w[g * HG:(g + 1) * HG, :].rearrange("h e -> (h e)").unsqueeze(1)
                                 ).then_inc(S["wc_in"], 16)
            sp.dma_start(wg[:], Wg.rearrange("(k p) e -> p k e", p=P)).then_inc(S["wg_in"], 16)
            sp.dma_start(xall[:, lead_a:NT, :], x_tiles[:, lead_a:NT, :]).then_inc(S["x_rest"], 16)
            sp.wait_ge(S["consts_pool"], 1)
            sp.dma_start(lists.rearrange("(p b) o -> p (b o)", p=P), pad).then_inc(S["lists_padded"], 16)
            for n, w in enumerate((Ws1, Ws3)):
                sp.dma_start(ws13[:, :, n, :], w.rearrange("(k p) f -> p k f", p=P)).then_inc(S["ws_in"], 16)
            sp.dma_start(ws2[:], Ws2.rearrange("(k p) c -> p k c", p=P)).then_inc(S["ws_in"], 16)
            for n, w in enumerate((W1, W3)):
                for k in range(KC):
                    sp.dma_start(w13[:, :, k, n, :], w[:, k * P:(k + 1) * P, :].rearrange("e p f -> p e f")
                                 ).then_inc(S["w13_in"], 16)

            def step(tile_of):
                if (a := tile_of(3)) is not None:
                    wait(sp, S["xn2_done"], a.t + 1)
                    sp.dma_start(xn2_rows.rearrange("(t p) c -> t p c", p=P)[bass.ds(a.t, 1)].rearrange("a p c -> (a p) c"),
                                 xn2[:, a.b, :]).then_inc(stored[a.b], 16)
            pipelined(sp, NT, 2, lead_a, 5, step)
            sp.wait_ge(S["o_ps"], NT)
            sp.wait_ge(S["ot_ps"], NT)
            sp.wait_ge(S["logits_ps"], NT)
            for b in range(2):
                sp.wait_ge(stored[b], 16 * NT // 2)
            sp.dma_start(w2[:], W2.rearrange("e p c -> p e c")).then_inc(S["w2_in"], 16)

            def store_step(tile_of):
                if (a := tile_of(6)) is not None:
                    wait(sp, S["y_done"], a.t + 1)
                    sp.dma_start(y_rows.rearrange("(t p) c -> t p c", p=P)[bass.ds(a.t, 1)].rearrange("a p c -> (a p) c"),
                                 y[:, a.ring, :]).then_inc(put[a.ring], 16)
            pipelined(sp, NJ, 4, 8, 8, store_step)

            def out_step(tile_of):
                if (a := tile_of(0)) is not None:
                    wait(sp, S["summed"], a.t + 1)
                    sp.dma_start(out_tiles[bass.ds(a.t, 1)].rearrange("a p c -> (a p) c"),
                                 xall[:, bass.ds(a.t, 1), :].rearrange("p a c -> p (a c)")).then_inc(final[a.b], 16)
            pipelined(sp, NT, 2, 2, 0, out_step)
            for b in range(2):
                sp.wait_ge(final[b], 16 * NT // 2)

        @block.gpsimd
        def _(pool):
            def pool_wait(sem, count, most=None):
                settled(pool, sem, count)

            pool.memset(pad, float(PAIRS)).then_inc(S["consts_pool"], 1)
            c = [1]

            def chain(ins):
                c[0] += 1
                ins.then_inc(S["consts_pool"], 1)
                pool.wait_ge(S["consts_pool"], c[0])

            chain(pool.memset(ident[:], 0.0))
            chain(pool.affine_select(out=ident[:], in_=ident[:], compare_op=ALU.not_equal, fill=1.0, base=0,
                                     pattern=[[-1, P]], channel_multiplier=1))
            chain(pool.memset(tri[:], 1.0))
            chain(pool.affine_select(out=tri[:], in_=tri[:], compare_op=ALU.is_ge, fill=0.0, base=0,
                                     pattern=[[1, P]], channel_multiplier=-1))
            chain(pool.memset(tri_bf[:], 1.0))
            chain(pool.affine_select(out=tri_bf[:], in_=tri_bf[:], compare_op=ALU.is_ge, fill=0.0, base=-1,
                                     pattern=[[1, P]], channel_multiplier=-1))
            chain(pool.memset(ones_bf[:], 1.0))
            chain(pool.memset(ones_f[:], 1.0))
            chain(pool.memset(head_mask[:], 1.0))
            for base, mult in ((0, 1), (d - 1, -1)):
                for g in range(KC):
                    v = head_mask[:, g, :].rearrange("p (h e) -> p h e", e=d)
                    chain(pool.affine_select(out=v, in_=v, compare_op=ALU.is_ge, fill=0.0, base=base,
                                             pattern=[[-d * mult, HG], [0, d]], channel_multiplier=mult))
            chain(pool.iota(par_i[:], pattern=[[0, 1]], base=0, channel_multiplier=1))
            chain(pool.iota(eidx_i[:], pattern=[[1, NJ // 4]], base=0, channel_multiplier=0))
            chain(pool.iota(pair_i[:], pattern=[[P * TOP_K, NT], [1, TOP_K]], base=0, channel_multiplier=TOP_K))
            chain(pool.iota(jc_i[:], pattern=[[P, 2]], base=0, channel_multiplier=1))
            chain(pool.memset(keep[:], 1.0))
            for s in range(B):
                chain(pool.memset(keep[:, s * NTB:s * NTB + 1], 0.0))
            chain(pool.memset(w_raw[:], 0.0))
            chain(pool.memset(w_bd[:], 0.0))
            chain(pool.memset(vp, 0.0))
            chain(pool.memset(mcum[:], 0.0))
            chain(pool.memset(minus_half[:], -0.5))
            chain(pool.memset(eps_col[:], RMS_EPS))
            assert c[0] == POOL_CONSTS
            pool.wait_ge(S["consts_dve"], 5)
            pool.wait_ge(S["lists_padded"], 16)

            def scatter(a, k):
                pool.indirect_dma_start(out=lists, out_offset=bass.IndirectOffsetOnAxis(ap=posi[:, a.b, k:k + 1], axis=0),
                                        in_=pid[:, a.b, k:k + 1], in_offset=None).then_inc(scattered[a.b], 16)

            def step(tile_of):
                if (a := tile_of(0)) is not None:
                    pool_wait(S["mean1"], a.t + 1)
                    pool_wait(S["xn_done"], a.t - 1)
                    pool.tensor_scalar(var1[:], mv1[:, a.b, 1:2], LN_EPS, None, ALU.add).then_inc(S["var1_done"], 1)
                    pool_wait(S["var1_done"], a.t + 1)
                    pool.tensor_tensor(rs1[:, a.b:a.b + 1], var1[:], minus_half[:], ALU.pow
                                       ).then_inc(S["rstd1"], 1)
                if (a := tile_of(5)) is not None:
                    pool_wait(scattered[a.b], (a.t - a.b) * 32, None)
                    pool.tensor_copy(pid[:, a.b, :], pair_all[:, bass.ds(a.t, 1), :].rearrange("p a k -> p (a k)")
                                     ).then_inc(S["pid_done"], 1)
                    pool_wait(S["pid_done"], a.t + 1)
                    pool_wait(S["pos_done"], a.t + 1)
                    scatter(a, 0)
                    scatter(a, 1)
                if (a := tile_of(3)) is not None:
                    pool_wait(S["mean2"], a.t + 1)
                    pool_wait(S["xn2_done"], a.t - 1)
                    pool.tensor_scalar(var2[:], mv2[:, a.b, 1:2], LN_EPS, None, ALU.add).then_inc(S["var2_done"], 1)
                    pool_wait(S["var2_done"], a.t + 1)
                    pool.tensor_tensor(rs2[:, a.b:a.b + 1], var2[:], minus_half[:], ALU.pow
                                       ).then_inc(S["rstd2"], 1)
                if (a := tile_of(5)) is not None:
                    scatter(a, 2)
                    scatter(a, 3)
                if (a := tile_of(0)) is not None:
                    pool_wait(S["guess_done"], a.t + 1)
                    pool_wait(S["v_done"], a.t - 1)
                    pool.tensor_scalar(msq[:], ss[:, a.b, :], RMS_EPS, None, ALU.add).then_inc(S["msq_done"], 1)
                    pool.tensor_tensor(gg[:], guess[:], guess[:], ALU.mult).then_inc(S["gg_done"], 1)
                    pool_wait(S["msq_done"], a.t + 1)
                    pool_wait(S["gg_done"], a.t + 1)
                    pool.tensor_tensor(mgg[:], msq[:], gg[:], ALU.mult).then_inc(S["mgg_done"], 1)
                    pool_wait(S["mgg_done"], a.t + 1)
                    pool.tensor_scalar(fac[:], mgg[:], -0.5, 1.5, ALU.mult, ALU.add).then_inc(S["fac_done"], 1)
                    pool_wait(S["fac_done"], a.t + 1)
                    pool.tensor_tensor(rr[:, a.b, :], guess[:], fac[:], ALU.mult).then_inc(S["rms_done"], 1)
                if (a := tile_of(1)) is not None:
                    for j in range(2):
                        pool_wait(S["s_copied"], 2 * a.t + j + 1)
                        v = s_sb[:, j].rearrange("p g r l -> p (g r) l")
                        pool.affine_select(out=v, in_=v, compare_op=ALU.is_ge, fill=0.0, base=0,
                                           pattern=[[0, 4], [1, P]], channel_multiplier=-1).then_inc(S["masked_pool"], 1)
            pipelined(pool, NT, 2, lead_a, 5, step)

            pool.wait_ge(S["tab_blk"], 1)
            for b in range(2):
                pool.wait_ge(scattered[b], 64 * NT // 2)
            for n, rows_n in enumerate((P, NJ - P)):
                pool.indirect_dma_start(out=lj[0:rows_n, n, :], out_offset=None, in_=lists_blocks,
                                        in_offset=bass.IndirectOffsetOnAxis(ap=blk_i[0:rows_n, n:n + 1], axis=0)
                                        ).then_inc(S["tab_lj_in"], 16)
            pool.wait_ge(S["tab_done"], 1)

            def expert_step(tile_of):
                if (a := tile_of(1)) is not None:
                    pool_wait(S["xT_ps"], a.t - 3)
                    pool_wait(S["bcopy"], a.t + 1)
                    pool.indirect_dma_start(out=xg[:, a.ring, :], out_offset=None, in_=xn2_rows,
                                            in_offset=bass.IndirectOffsetOnAxis(ap=tok_b[:, a.ring:a.ring + 1], axis=0)
                                            ).then_inc(gathered[a.ring], 16)
            pipelined(pool, NJ, 4, 8, 8, expert_step)

            for b in range(4):
                pool.wait_ge(put[b], 16 * NJ // 4)
            pool.wait_ge(S["hb_ps"], NJ)

            def rows_step(tile_of):
                if (a := tile_of(0)) is not None:
                    pool_wait(S["summed"], a.t - 3)
                    pool_wait(S["rcopy"], a.t + 1)
                    for k in range(TOP_K):
                        pool.indirect_dma_start(out=rows[:, a.ring, k, :], out_offset=None, in_=y_rows,
                                                in_offset=bass.IndirectOffsetOnAxis(ap=row_b[:, a.ring, k:k + 1], axis=0)
                                                ).then_inc(rows_in[a.ring], 16)
            pipelined(pool, NT, 4, 4, 0, rows_step)

        @block.scalar
        def _(act):
            for k in range(KC):
                act.wait_ge(S["wt_ps"], k + 1)
                act.copy(wqv[:, k, :], (pT0, pT1)[k][:]).then_inc(S["wt_done"], 1)

            def step(tile_of):
                if (a := tile_of(4)) is not None:
                    wait(act, S["nmx_done"], a.t + 1)
                    wait(act, S["prob_done"], a.t - 1)
                    act.activation(ex[:, a.b, :], lg[:, a.b, :], ACT.Exp, bias=nmx[:, a.b:a.b + 1], scale=1.0,
                                   accum_out=se[:, a.b:a.b + 1]).then_inc(S["exp_done"], 1)
                if (a := tile_of(2)) is not None:
                    wait(act, S["o_ps"], a.t + 1)
                    wait(act, S["ot_ps"], a.t - 1)
                    for g in range(KC):
                        last = act.activation(oT[:, a.b, g, :], pO[:, g * P:(g + 1) * P], ACT.Copy, scale=wvc[:, g:g + 1])
                    last.then_inc(S["oT_done"], 1)
                if (a := tile_of(0)) is not None:
                    wait(act, S["xnT_ps"], a.t + 1)
                    wait(act, S["qv_ps"], a.t - 1)
                    wait(act, S["scores_ps"], 4 * (a.t - 1))
                    act.copy(xnT[:, a.b], pT0[:, 0:D].rearrange("p (g m) -> p g m", g=KC)).then_inc(S["xnT_done"], 1)
                if (a := tile_of(1)) is not None:
                    wait(act, S["qT_ps"], a.t + 1)
                    wait(act, S["scores_ps"], 4 * a.t)
                    for r in range(2):
                        for g in range(KC):
                            last = act.activation(qm[:, r, g, :], pT1[:, g * P:(g + 1) * P], ACT.Copy,
                                                  scale=mwq[:, r, g:g + 1])
                    last.then_inc(S["qm_done"], 1)
                    wait(act, S["o_ps"], a.t)
                    act.copy(qT, pT1[:, 0:D].rearrange("p (g m) -> p g m", g=KC)).then_inc(S["qT_done"], 1)
                if (a := tile_of(0)) is not None:
                    wait(act, S["qv_ps"], a.t + 1)
                    wait(act, S["ss_done"], a.t)
                    act.activation(sq, pQV[:], ACT.Square, scale=float(d) ** -0.5).then_inc(S["sq_done"], 1)
                    wait(act, S["ss_done"], a.t + 1)
                    act.activation(lnm[:], ss[:, a.b, :], ACT.Ln, bias=eps_col[:]).then_inc(S["ln_done"], 1)
                    wait(act, S["ln_done"], a.t + 1)
                    wait(act, S["rms_done"], a.t)
                    act.activation(guess[:], lnm[:], ACT.Exp, scale=-0.5).then_inc(S["guess_done"], 1)
                if (a := tile_of(3)) is not None:
                    wait(act, S["x2T_ps"], a.t + 1)
                    wait(act, S["logits_ps"], a.t - 1)
                    src = pT0[:, 0:D].rearrange("p (g m) -> p g m", g=KC)
                    act.copy(x2T[:, a.b], src)
                    act.copy(x2T_all[:].rearrange("p k (t l) -> p k t l", l=P)[:, :, bass.ds(a.t, 1), :].rearrange("p k a l -> p k (a l)"),
                             src).then_inc(S["x2T_done"], 1)
                if (a := tile_of(1)) is not None:
                    for j in range(2):
                        wait(act, S["scores_ps"], 4 * a.t + j + 1)
                        wait(act, S["o_ps"], a.t)
                        act.copy(s_sb[:, j].rearrange("p g r l -> p (g r l)"), pS[j][:]).then_inc(S["s_copied"], 1)
                if (a := tile_of(4)) is not None:
                    wait(act, S["rank_ps"], a.t + 1)
                    wait(act, S["placed_done"], a.t)
                    act.copy(rk[:], pT1[:, 0:E]).then_inc(S["rk_done"], 1)
                if (a := tile_of(3)) is not None:
                    wait(act, S["logits_ps"], a.t + 1)
                    wait(act, S["nmx_done"], a.t - 1)
                    wait(act, S["exp_done"], a.t - 1)
                    act.copy(lg[:, a.b, :], pO[:, D:D + E]).then_inc(S["lg_done"], 1)
            act.wait_ge(S["wc_in"], 64)
            act.wait_ge(S["consts_pool"], POOL_CONSTS)
            act.wait_ge(S["consts_dve"], 8)
            act.preload_act_table_set("natural_log_exp_and_others")
            pipelined(act, NT, 2, lead_a, 5, step)

            act.preload_act_table(ACT.Silu)

            def expert_step(tile_of):
                if (a := tile_of(4)) is not None:
                    wait(act, S["xT_ps"], a.t + 1)
                    wait(act, S["hb_ps"], a.t - 1)
                    act.copy(xgT[:, a.b], pT0[:, 0:D].rearrange("p (g m) -> p g m", g=KC)).then_inc(S["xT_done"], 1)
                if (a := tile_of(5)) is not None:
                    wait(act, S["hb_ps"], a.t + 1)
                    wait(act, S["ge_done"], a.t - 1)
                    act.activation(sge[:, a.b, :], pS[a.b][:, 0:F], ACT.Silu).then_inc(S["sge_done"], 1)
                if (a := tile_of(6)) is not None:
                    wait(act, S["y_ps"], a.t + 1)
                    wait(act, put[a.ring], (a.t - a.ring) * 4)
                    act.copy(y[:, a.ring, :], pS[2 + a.b][:, 0:D]).then_inc(S["y_done"], 1)
            pipelined(act, NJ, 4, 8, 8, expert_step)
            for b in range(4):
                act.wait_ge(put[b], 16 * NJ // 4)

            def shared_step(tile_of):
                if (a := tile_of(0)) is not None:
                    for m in range(FC):
                        wait(act, S["h_ps"], FC * a.t + m + 1)
                        wait(act, S["gsh_done"], FC * (a.t - 1) + m + 1)
                        act.activation(sg[:, m, :], pS[2 * m][:], ACT.Silu).then_inc(S["silu_done"], 1)
            pipelined(act, NG, 2, 2, 1, shared_step)

        @block.tensor
        def _(pe):
            pe.wait_ge(S["w_in"], 32)
            pe.wait_ge(S["consts_pool"], POOL_CONSTS)
            for k in range(KC):
                for n, w in enumerate((wq_in, wv_in)):
                    for o in range(KC):
                        at = n * D + o * P
                        last = pe.transpose((pT0, pT1)[k][:, at:at + P], w[:, o, k * P:(k + 1) * P], ident[:])
                last.then_inc(S["wt_ps"], 1)
            pe.wait_ge(S["wt_done"], KC)
            pe.wait_ge(S["consts_dve"], 5)
            pe.wait_ge(S["wg_in"], 16)

            def step(tile_of):
                if (a := tile_of(2)) is not None:
                    wait(pe, S["qT_done"], a.t + 1)
                    wait(pe, S["state_done"], a.t)
                    wait(pe, S["oT_done"], a.t)
                    wait(pe, S["lg_done"], a.t - 1)
                    wait(pe, S["masked"], 2 * a.t + 2)
                    wait(pe, S["masked_pool"], 2 * a.t + 2)
                    for g in range(KC):
                        pe.matmul(pO[:, g * P:(g + 1) * P], w_bd[:, a.b, g * P:(g + 1) * P], qT[:, g, :],
                                  start=(g == 0), stop=False, skip_group_check=True)
                    for g in range(KC):
                        for r in range(2):
                            for j in range(4):
                                last = pe.matmul(pO[32 * j:32 * j + 32, g * P:(g + 1) * P],
                                                 vp[:, a.b, 4 * g + j, r:r + 2, :], s_sb[:, j, g, r, :],
                                                 start=False, stop=(r == 1), skip_group_check=True)
                    last.then_inc(S["o_ps"], 1)
                if (a := tile_of(3)) is not None:
                    wait(pe, S["oT_done"], a.t + 1)
                    wait(pe, S["rk_done"], a.t - 1)
                    wait_at_ends(pe, S["qT_done"], a.t + 2, NT)
                    wait_at_ends(pe, S["x2_done"], a.t)
                    for g in range(KC):
                        last = pe.transpose(pT1[:, g * P:(g + 1) * P], oT[:, a.b, g, :], ident[:])
                    last.then_inc(S["ot_ps"], 1)
                if (a := tile_of(0)) is not None:
                    wait(pe, S["xn_done"], a.t + 1)
                    wait(pe, S["x2T_done"], a.t - 3)
                    wait_at_ends(pe, S["xnT_done"], a.t)
                    wait_at_ends(pe, S["raw_done"], a.t - 1)
                    for g in range(KC):
                        last = pe.transpose(pT0[:, g * P:(g + 1) * P], xn[:, a.b, g * P:(g + 1) * P], ident[:])
                    last.then_inc(S["xnT_ps"], 1)
                if (a := tile_of(1)) is not None:
                    wait(pe, S["qn_done"], a.t + 1)
                    wait(pe, S["x2_done"], a.t - 1)
                    wait_at_ends(pe, S["qT_done"], a.t)
                    for g in range(KC):
                        last = pe.transpose(pT1[:, g * P:(g + 1) * P], qn[:, a.b, g * P:(g + 1) * P], ident[:])
                    last.then_inc(S["qT_ps"], 1)
                    wait(pe, S["v_done"], a.t + 1)
                    wait(pe, S["xnT_done"], a.t + 2, NT)
                    wait_at_ends(pe, S["x2T_done"], a.t - 2)
                    for g in range(KC):
                        last = pe.matmul(pT0[:, g * P:(g + 1) * P], xn[:, a.b, g * P:(g + 1) * P],
                                         vp[:, a.b, 4 * g:4 * g + 4, 0:3:2, :], start=True, stop=True)
                    last.then_inc(S["state_ps"], 1)
                if (a := tile_of(0)) is not None:
                    wait(pe, S["xnT_done"], a.t + 1)
                    wait(pe, S["v_done"], a.t)
                    for k in range(KC):
                        last = pe.matmul(pQV[:], xnT[:, a.b, k, :], wqv[:, k, :], start=(k == 0), stop=(k == KC - 1))
                    last.then_inc(S["qv_ps"], 1)
                if (a := tile_of(1)) is not None:
                    wait(pe, S["qm_done"], a.t + 1)
                    wait(pe, S["masked"], 2 * a.t)
                    wait(pe, S["s_copied"], 2 * a.t)
                for g in range(KC):
                    if (a := tile_of(1)) is not None:
                        for j in range(4):
                            last = pe.matmul(pS[j][:, g * 256:(g + 1) * 256], xnT[32 * j:32 * j + 32, a.b, g, :],
                                             qm[32 * j:32 * j + 32, :, g, :], start=(g == 0), stop=True,
                                             skip_group_check=True)
                            if g == KC - 1:
                                last.then_inc(S["scores_ps"], 1)
                    if g == 0 and (a := tile_of(3)) is not None:
                        wait(pe, S["xn2_done"], a.t + 1)
                        wait(pe, S["raw_done"], a.t + 3, NT)
                        wait_at_ends(pe, S["x2T_done"], a.t)
                        for c in range(KC):
                            last = pe.transpose(pT0[:, c * P:(c + 1) * P], xn2[:, a.b, c * P:(c + 1) * P], ident[:])
                        last.then_inc(S["x2T_ps"], 1)
                if (a := tile_of(4)) is not None:
                    wait(pe, S["mask_done"], a.t + 1)
                    wait(pe, S["mcum_done"], a.t)
                    wait(pe, S["qT_done"], a.t + 4, NT)
                    wait_at_ends(pe, S["x2_done"], a.t + 2, NT)
                    wait_at_ends(pe, S["rk_done"], a.t)
                    pe.matmul(pT1[:, 0:E], tri_bf[:], mask[:, a.b, :], start=True, stop=False)
                    pe.matmul(pT1[:, 0:E], ones_bf[:], mcum[:, a.b, :], start=False, stop=True).then_inc(S["rank_ps"], 1)
                if (a := tile_of(3)) is not None:
                    wait(pe, S["x2T_done"], a.t + 1)
                    wait(pe, S["oT_done"], a.t + 2, NT)
                    wait_at_ends(pe, S["lg_done"], a.t)
                    for k in range(KC):
                        last = pe.matmul(pO[:, D:D + E], x2T[:, a.b, k, :], wg[:, k, :], start=(k == 0), stop=(k == KC - 1))
                    last.then_inc(S["logits_ps"], 1)
            pipelined(pe, NT, 2, lead_a, 5, step)

            pe.wait_ge(S["mcum_done"], NT)
            pe.wait_ge(S["rk_done"], NT)
            pe.matmul(pT1[:, 0:E], ones_bf[:], mcum[:, NT % 2, :], start=True, stop=True).then_inc(S["cnt_ps"], 1)
            pe.wait_ge(S["tab_blk"], 1)
            for n in range(2):
                last = pe.matmul(pT1[0:1, n * P:(n + 1) * P], ejc[:, n:n + 1], ident[:], start=True, stop=True)
            last.then_inc(S["erow_ps"], 1)
            pe.wait_ge(S["tab_lj_in"], 32)
            pe.transpose(pT0[:, 0:P], lj[:, 0, :], ident[:])
            pe.transpose(pT0[:, P:NJ], lj[0:NJ - P, 1, :], ident[0:NJ - P, 0:NJ - P]).then_inc(S["tab_ps"], 1)
            pe.wait_ge(S["tab_done"], 1)
            pe.wait_ge(S["erow_done"], 1)
            pe.wait_ge(S["w13_in"], 16 * 2 * KC)
            pe.wait_ge(S["w2_in"], 16)
            pe.wait_ge(S["masked"], 2 * NT)

            number = [pe.alloc_register(f"expert{n}") for n in range(4)]

            def load_number(a):
                pe.reg_load(number[a.ring], erow[0:1, bass.ds(a.t, 1)])

            def expert_of(a):
                return nc.s_assert_within(pe.snap(number[a.ring]), 0, E - 1, skip_runtime_bounds_check_because="the table holds experts 0 .. E-1 only")

            def expert_step(tile_of):
                if (a := tile_of(4)) is not None:
                    wait(pe, gathered[a.ring], (a.t - a.ring) * 4 + 16)
                    wait(pe, S["xT_done"], a.t)
                    for g in range(KC):
                        last = pe.transpose(pT0[:, g * P:(g + 1) * P], xg[:, a.ring, g * P:(g + 1) * P], ident[:])
                    last.then_inc(S["xT_ps"], 1)
                if (a := tile_of(6)) is not None:
                    wait(pe, S["ge_done"], a.t + 1)
                    wait(pe, S["gT_done"], a.t)
                    pe.transpose(pT1[:, 0:P], ge[:, a.b, :], ident[:]).then_inc(S["gT_ps"], 1)
                if (a := tile_of(5)) is not None:
                    e = expert_of(a)
                    wait(pe, S["xT_done"], a.t + 1)
                    wait(pe, S["ge_done"], a.t - 1)
                    for k in range(KC):
                        last = pe.matmul(pS[a.b][:, 0:2 * F], xgT[:, a.b, k, :],
                                         w13[:, bass.ds(e, 1), k, :, :].rearrange("p a n f -> p (a n f)"),
                                         start=(k == 0), stop=(k == KC - 1))
                    last.then_inc(S["hb_ps"], 1)
                if (a := tile_of(4)) is not None:
                    load_number(a)
                if (a := tile_of(6)) is not None:
                    e = expert_of(a)
                    wait(pe, S["gT_done"], a.t + 1)
                    wait(pe, S["y_done"], a.t - 1)
                    pe.matmul(pS[2 + a.b][:, 0:D], geT[:, a.b, :],
                              w2[:, bass.ds(e, 1), :].rearrange("p a c -> p (a c)"), start=True, stop=True
                              ).then_inc(S["y_ps"], 1)
            pipelined(pe, NJ, 4, 8, 8, expert_step)
            pe.wait_ge(S["y_done"], NJ)

            pe.wait_ge(S["ws_in"], 48)

            def shared_step(tile_of):
                if (a := tile_of(0)) is not None:
                    for m in range(FC):
                        wait(pe, S["gsh_done"], FC * (a.t - 1) + m + 1)
                        for n in range(2):
                            for k in range(KC):
                                last = pe.matmul(pS[2 * m + n][:], ws13[:, k, n, m * P:(m + 1) * P],
                                                 x2T_all[:, k, bass.ds(a.t * TG, TG)], start=(k == 0), stop=(k == KC - 1))
                        last.then_inc(S["h_ps"], 1)
                if (a := tile_of(1)) is not None:
                    wait(pe, S["gsh_done"], FC * (a.t + 1))
                    for q in range(TG // P):
                        wait(pe, S["z_done"], 4 * a.t + q - 1)
                        for m in range(FC):
                            last = pe.matmul((pQV, pO)[q % 2][:, 0:D], gsh[:, a.b, m, q * P:(q + 1) * P], ws2[:, m, :],
                                             start=(m == 0), stop=(m == FC - 1))
                        last.then_inc(S["z_ps"], 1)
            pipelined(pe, NG, 2, 4, 1, shared_step)

        @block.vector
        def _(dve):
            dve.wait_ge(S["consts_pool"], POOL_CONSTS)
            dve.wait_ge(S["wc_in"], 64)
            c = [0]

            def chain(ins):
                c[0] += 1
                ins.then_inc(S["consts_dve"], 1)
                dve.wait_ge(S["consts_dve"], c[0])

            chain(dve.tensor_scalar(par_i[:], par_i[:], 4, 1, ALU.logical_shift_right, ALU.bitwise_and))
            chain(dve.tensor_copy(par_f[:, 1:2], par_i[:]))
            chain(dve.tensor_scalar(par_f[:, 0:1], par_f[:, 1:2], -1.0, 1.0, ALU.mult, ALU.add))
            chain(dve.tensor_copy(eidx[:], eidx_i[:]))
            chain(dve.tensor_copy(pair_all[:].rearrange("p t k -> p (t k)"), pair_i[:]))
            chain(dve.tensor_scalar(ebase[:], eidx[:, 0:E], float(T), None, ALU.mult))
            for r in range(2):
                chain(dve.tensor_scalar(mwq[:, r, :], wqc[:], par_f[:, r:r + 1], None, ALU.mult))
            for g in range(KC):
                chain(dve.tensor_scalar(head_mask[:, g, :], head_mask[:, g, :], wqc[:, g:g + 1], None, ALU.mult))
            chain(dve.tensor_copy(jc[:], jc_i[:]))

            def x_tile(a):
                return xall[:, bass.ds(a.t, 1), :].rearrange("p a c -> p (a c)")

            def step(tile_of):
                a0, a1, a3, a4, a5 = (tile_of(s) for s in (0, 1, 3, 4, 5))
                if a1 is not None:
                    wait(dve, S["rms_done"], a1.t + 1)
                    wait(dve, S["qT_ps"], a1.t - 1)
                    dve.tensor_tensor(qn[:, a1.b, :].rearrange("p (h e) -> p h e", e=d), pQV[:, 0:D].rearrange("p (h e) -> p h e", e=d),
                                      rr[:, a1.b, 0:H].unsqueeze(2).to_broadcast([P, H, d]), ALU.mult).then_inc(S["qn_done"], 1)
                    wait(dve, S["o_ps"], a1.t - 1)
                    dve.tensor_tensor(vp[:, a1.b, :, 0:3:2, :], pQV[:, D:2 * D].rearrange("p (n r e) -> p n r e", r=2, e=d),
                                      rr[:, a1.b, H:2 * H].rearrange("p (n r) -> p n r", r=2).unsqueeze(3).to_broadcast([P, NP_, 2, d]),
                                      ALU.mult).then_inc(S["v_done"], 1)
                if a0 is not None:
                    dve.bn_stats(st[:], x_tile(a0)).then_inc(S["stats1"], 1)
                if a5 is not None:
                    wait(dve, S["rk_done"], a5.t + 1)
                    dve.tensor_tensor(place[:], rk[:], ebase[:], ALU.add).then_inc(S["placed_done"], 1)
                if a4 is not None:
                    settled(dve, S["lg_done"], a4.t + 1)
                    dve.max(m8[:], lg[:, a4.b, :]).then_inc(S["max_done"], 1)
                if a0 is not None:
                    settled(dve, S["stats1"], a0.t + 1)
                    dve.bn_aggr(mv1[:, a0.b, :], st[:]).then_inc(S["mean1"], 1)
                if a5 is not None:
                    wait(dve, S["placed_done"], a5.t + 1)
                    dve.tensor_tensor(ohr[:], oh[:], place[:].unsqueeze(1).to_broadcast([P, TOP_K, E]), ALU.mult
                                      ).then_inc(S["place_done"], 1)
                if a4 is not None:
                    wait(dve, S["max_done"], a4.t + 1)
                    wait(dve, S["exp_done"], a4.t - 1)
                    dve.tensor_scalar(nmx[:, a4.b:a4.b + 1], m8[:, 0:1], -1.0, None, ALU.mult).then_inc(S["nmx_done"], 1)
                if a5 is not None:
                    wait(dve, S["place_done"], a5.t + 1)
                    dve.tensor_reduce(pos[:], ohr[:], AX_X, ALU.add).then_inc(S["pos_kept"], 1)
                if a0 is not None:
                    wait(dve, S["rstd1"], a0.t + 1)
                    wait(dve, S["state_ps"], a0.t - 1)
                    dve.tensor_scalar(xn[:, a0.b, :], x_tile(a0), mv1[:, a0.b, 0:1], rs1[:, a0.b:a0.b + 1],
                                      ALU.subtract, ALU.mult).then_inc(S["xn_done"], 1)
                if a5 is not None:
                    wait(dve, S["pos_kept"], a5.t + 1)
                    wait(dve, scattered[a5.b], (a5.t - a5.b) * 32)
                    dve.tensor_copy(posi[:, a5.b, :], pos[:]).then_inc(S["pos_done"], 1)
                    dve.tensor_copy(posi_all[:, bass.ds(a5.t, 1), :].rearrange("p a k -> p (a k)"), pos[:])
                if a4 is not None:
                    t1 = a4.t + 1
                    wait(dve, S["exp_done"], t1)
                    dve.reciprocal(rin[:], se[:, a4.b:a4.b + 1]).then_inc(S["rin_done"], 1)
                if a3 is not None:
                    wait(dve, S["ot_ps"], a3.t + 1)
                    dve.tensor_tensor(x_tile(a3), x_tile(a3), pT1[:, 0:D], ALU.add).then_inc(S["x2_done"], 1)
                if a4 is not None:
                    wait(dve, S["rin_done"], t1)
                    dve.tensor_scalar(prob[:], ex[:, a4.b, :], rin[:], None, ALU.mult).then_inc(S["prob_done"], 1)
                if a3 is not None:
                    settled(dve, S["x2_done"], a3.t + 1)
                    dve.bn_stats(st2[:], x_tile(a3)).then_inc(S["stats2"], 1)
                if a4 is not None:
                    settled(dve, S["prob_done"], t1)
                    dve.max(t8[:], prob[:]).then_inc(S["top_done"], 1)
                if a3 is not None:
                    settled(dve, S["stats2"], a3.t + 1)
                    dve.bn_aggr(mv2[:, a3.b, :], st2[:]).then_inc(S["mean2"], 1)
                if a4 is not None:
                    settled(dve, S["top_done"], t1)
                    dve.max_index(ix[:], t8[:], prob[:]).then_inc(S["ix_done"], 1)
                    dve.tensor_copy(wts[:, bass.ds(a4.t, 1), :].rearrange("p a k -> p (a k)"), t8[:, 0:TOP_K])
                if a1 is not None:
                    wait(dve, S["state_ps"], a1.t + 1)
                    dve.scalar_tensor_tensor(out=w_raw[:], in0=w_raw[:], scalar=keep[:, bass.ds(a1.t, 1)], in1=pT0[:, 0:D],
                                             op0=ALU.mult, op1=ALU.add).then_inc(S["raw_done"], 1)
                if a4 is not None:
                    wait(dve, S["ix_done"], t1)
                    dve.tensor_copy(ixf[:], ix[:, 0:TOP_K]).then_inc(S["ixf_done"], 1)
                if a1 is not None:
                    wait(dve, S["raw_done"], a1.t + 1)
                    wait(dve, S["o_ps"], a1.t)
                    dve.scalar_tensor_tensor(out=w_bd[:, 1 - a1.b, :], in0=w_raw[:], scalar=keep[:, bass.ds(a1.t + 1, 1)],
                                             in1=head_mask[:].rearrange("p g c -> p (g c)"), op0=ALU.mult, op1=ALU.mult
                                             ).then_inc(S["state_done"], 1)
                if a4 is not None:
                    wait(dve, S["ixf_done"], t1)
                    dve.tensor_tensor(oh[:], eidx[:, 0:E].unsqueeze(1).to_broadcast([P, TOP_K, E]),
                                      ixf[:].unsqueeze(2).to_broadcast([P, TOP_K, E]), ALU.is_equal).then_inc(S["oh_done"], 1)
                if a3 is not None:
                    wait(dve, S["rstd2"], a3.t + 1)
                    wait(dve, S["x2T_ps"], a3.t - 1)
                    wait(dve, stored[a3.b], (a3.t - a3.b) * 8)
                    dve.tensor_scalar(xn2[:, a3.b, :], x_tile(a3), mv2[:, a3.b, 0:1], rs2[:, a3.b:a3.b + 1],
                                      ALU.subtract, ALU.mult).then_inc(S["xn2_done"], 1)
                if a4 is not None:
                    wait(dve, S["oh_done"], t1)
                    with nc.allow_low_precision("0 and 1 are exact"):
                        dve.tensor_reduce(mask[:, a4.b, :], oh[:].rearrange("p k e -> p e k"), AX_X, ALU.add
                                          ).then_inc(S["mask_done"], 1)
                if a0 is not None:
                    wait(dve, S["sq_done"], a0.t + 1)
                    wait(dve, S["rms_done"], a0.t - 1)
                    dve.tensor_reduce(ss[:, a0.b, :], sq.rearrange("p (h e) -> p h e", e=d), AX_X, ALU.add
                                      ).then_inc(S["ss_done"], 1)
                if a4 is not None:
                    wait(dve, S["mask_done"], t1)
                    wait(dve, S["rank_ps"], a4.t)
                    dve.tensor_tensor(mcum[:, 1 - a4.b, :], mcum[:, a4.b, :], mask[:, a4.b, :], ALU.add
                                      ).then_inc(S["mcum_done"], 1)
                if a1 is not None:
                    for j in (2, 3):
                        wait(dve, S["scores_ps"], 4 * a1.t + j + 1)
                        wait(dve, S["o_ps"], a1.t)
                        dve.tensor_tensor(s_sb[:, j].rearrange("p g r l -> p (g r) l"), pS[j][:].rearrange("p (n l) -> p n l", l=P),
                                          tri[:].unsqueeze(1).to_broadcast([P, 4, P]), ALU.mult).then_inc(S["masked"], 1)

            dve.wait_ge(S["x_first"], 16)
            pipelined(dve, NT, 2, lead_a, 5, step, lambda: dve.wait_ge(S["x_rest"], 16))

            r = [0]

            def tab(ins, done="tabs"):
                r[0] += 1
                ins.then_inc(S["tabs"], 1)
                dve.wait_ge(S["tabs"], r[0])

            dve.wait_ge(S["cnt_ps"], 1)
            tab(dve.tensor_scalar(cnt_i[:], pT1[:, 0:E], float(P - 1), None, ALU.add))
            tab(dve.tensor_scalar(nt_i[:], cnt_i[:], 7, None, ALU.logical_shift_right))
            tab(dve.tensor_copy(ntf[:], nt_i[:]))
            tab(dve.tensor_tensor_scan(endt[:], ones_f[:], ntf[:], 0.0, ALU.mult, ALU.add))
            for n in range(2):
                tab(dve.tensor_scalar(behind[:, n, :], endt[:], jc[:, n:n + 1], None, ALU.is_le))
            tab(dve.tensor_reduce(ej[:], behind[:], AX_X, ALU.add))
            tab(dve.tensor_tensor(bnt[:], behind[:], ntf[:].unsqueeze(1).to_broadcast([P, 2, E]), ALU.mult))
            tab(dve.tensor_reduce(stj[:], bnt[:], AX_X, ALU.add))
            tab(dve.tensor_tensor(jrel[:], jc[:], stj[:], ALU.subtract))
            tab(dve.scalar_tensor_tensor(out=blk[:], in0=ej[:], scalar=float(NBE), in1=jrel[:], op0=ALU.mult, op1=ALU.add))
            tab(dve.tensor_scalar(blk_i[:], blk[:], float(NB), None, ALU.min))
            tab(dve.tensor_scalar(ejc[:], ej[:], float(E - 1), None, ALU.min))
            dve.tensor_copy(jrel[:], jc[:]).then_inc(S["tab_blk"], 1)
            flat_w = wts[:].rearrange("p t k -> p (t k)")
            tab(dve.tensor_scalar(rank_i[:], posi_all[:].rearrange("p t k -> p (t k)"), T - 1, None, ALU.bitwise_and))
            tab(dve.tensor_scalar(inside[:], rank_i[:], float(CAP), None, ALU.is_lt))
            tab(dve.tensor_tensor(flat_w, flat_w, inside[:], ALU.mult))

            tab(dve.memset(shift[:], 0.0))
            tab(dve.tensor_tensor(shift[:, 0:E], endt[:], ntf[:], ALU.subtract))
            tab(dve.scalar_tensor_tensor(out=shift[:, 0:E], in0=shift[:, 0:E], scalar=float(P), in1=ebase[:], op0=ALU.mult,
                                         op1=ALU.subtract))
            flat_pos = posi_all[:].rearrange("p t k -> p (t k)")
            tab(dve.tensor_scalar(place_e[:], flat_pos, T.bit_length() - 1, None, ALU.logical_shift_right))
            tab(dve.tensor_copy(place_ef[:], place_e[:]))
            tab(dve.tensor_copy(rowf[:], flat_pos))
            dve.wait_ge(S["erow_ps"], 1)
            dve.tensor_copy(erow[:], pT1[0:1, 0:256]).then_inc(S["erow_done"], 1)
            dve.wait_ge(S["tab_ps"], 1)
            tab(dve.tensor_copy(slot_i[:], pT0[:, 0:NJ]))
            tab(dve.tensor_scalar(tok_i[:], slot_i[:], 2, None, ALU.logical_shift_right))
            tab(dve.tensor_scalar(tok_i[:], tok_i[:], float(T - 1), None, ALU.min))
            dve.engine_nop().then_inc(S["tab_done"], 1)

            def expert_step(tile_of):
                if (a := tile_of(0)) is not None and a.ring == 0:
                    wait(dve, S["row_tab"], a.turn)
                    dve.tensor_scalar(moved[:], place_ef[:], eidx[:, bass.ds(a.turn, 1)], shift[:, bass.ds(a.turn, 1)],
                                      ALU.is_equal, ALU.mult).then_inc(S["moved_done"], 1)
                if (a := tile_of(0)) is not None and a.ring == 2:
                    wait(dve, S["moved_done"], a.turn + 1)
                    dve.tensor_tensor(rowf[:], rowf[:], moved[:], ALU.add).then_inc(S["row_tab"], 1)
                if (a := tile_of(0)) is not None:
                    wait(dve, gathered[a.ring], (a.t - a.ring) * 4)
                    dve.tensor_copy(tok_b[:, a.ring:a.ring + 1], tok_i[:, bass.ds(a.t, 1)]).then_inc(S["bcopy"], 1)
                if (a := tile_of(6)) is not None:
                    wait(dve, S["gT_ps"], a.t + 1)
                    wait(dve, S["y_ps"], a.t - 1)
                    dve.tensor_copy(geT[:, a.b, :], pT1[:, 0:P]).then_inc(S["gT_done"], 1)
                if (a := tile_of(5)) is not None:
                    wait(dve, S["sge_done"], a.t + 1)
                    wait(dve, S["gT_ps"], a.t - 1)
                    dve.tensor_tensor(ge[:, a.b, :], sge[:, a.b, :], pS[a.b][:, F:2 * F], ALU.mult).then_inc(S["ge_done"], 1)
            pipelined(dve, NJ, 4, 8, 8, expert_step)

            tab(dve.tensor_copy(row_i[:].rearrange("p t k -> p (t k)"), rowf[:]))
            QT_ = TG // P
            for t in range(QT_):
                dve.tensor_copy(row_b[:, t, :], row_i[:, t, :]).then_inc(S["rcopy"], 1)

            def group_step(tile_of):
                if (a := tile_of(0)) is not None:
                    for m in range(FC):
                        wait(dve, S["silu_done"], FC * a.t + m + 1)
                        wait(dve, S["z_ps"], QT_ * (a.t - 1))
                        dve.tensor_tensor(gsh[:, a.b, m, :], sg[:, m, :], pS[2 * m + 1][:], ALU.mult).then_inc(S["gsh_done"], 1)
                if (a := tile_of(1)) is not None:
                    for q in range(QT_):
                        t = a.t * QT_ + q
                        xt = xall[:, bass.ds(t, 1), :].rearrange("p a c -> p (a c)")
                        wait(dve, S["z_ps"], t + 1)
                        dve.tensor_tensor(xt, xt, (pQV, pO)[q % 2][:, 0:D], ALU.add).then_inc(S["z_done"], 1)
                        wait(dve, S["z_done"], t + 1)
                        wait(dve, rows_in[q], 16 * TOP_K * (a.t + 1))
                        for k in range(TOP_K):
                            ins = dve.scalar_tensor_tensor(out=xt, in0=rows[:, q, k, :],
                                                           scalar=wts[:, bass.ds(t, 1), k:k + 1].rearrange("p a k -> p (a k)"),
                                                           in1=xt, op0=ALU.mult, op1=ALU.add)
                            if k < TOP_K - 1:
                                ins.then_inc(S["added"], 1)
                                wait(dve, S["added"], (TOP_K - 1) * t + k + 1)
                            else:
                                ins.then_inc(S["summed"], 1)
                        if not (isinstance(t, int) and t + QT_ >= NT):
                            dve.tensor_copy(row_b[:, q, :], row_i[:, bass.ds(t + QT_, 1), :].rearrange("p a k -> p (a k)")
                                            ).then_inc(S["rcopy"], 1)
            pipelined(dve, NG, 2, 2, 1, group_step)


_INS = ["L0_attn_X", "L0_attn_Wq", "L0_attn_Wv", "L0_attn_q_norm_w", "L0_attn_v_norm_w", "L0_ffn_Wg", "L0_ffn_W1",
        "L0_ffn_W2", "L0_ffn_W3", "L0_ffn_Ws1", "L0_ffn_Ws2", "L0_ffn_Ws3"]


def kernel(**inputs):
    import numpy as _np
    import concourse.bacc as _bacc
    from concourse import mybir as _mybir
    from concourse.bass_utils import run_bass_kernel_spmd as _run

    nc = _bacc.Bacc("TRN2", target_bir_lowering=False, num_devices=1)
    arrays, args = {}, []
    for name in _INS:
        a = _np.ascontiguousarray(inputs[name])
        arrays[f"in_{name}"] = a
        args.append(nc.dram_tensor(f"in_{name}", a.shape, _mybir.dt.from_np(a.dtype), kind="ExternalInput").ap())
    shape = inputs["L0_attn_X"].shape
    args.append(nc.dram_tensor("out", shape, _mybir.dt.float32, kind="ExternalOutput").ap())
    build(nc, *args)
    r = _run(nc, [arrays], core_ids=[0])
    return r.results[0]["out"]
```

```python
from contextlib import ExitStack

import concourse.bass as bass
from concourse import mybir

F32 = mybir.dt.float32
BF16 = mybir.dt.bfloat16
I32 = mybir.dt.int32
U32 = mybir.dt.uint32
ALU = mybir.AluOpType
ACT = mybir.ActivationFunctionType
AX_X = mybir.AxisListType.X

P = 128
LN_EPS = 1e-5
RMS_EPS = 1e-8
TOP_K = 4
CAP_FACTOR = 4


class Tile:

    def __init__(self, t, ring, turn=None):
        self.t, self.ring = t, ring
        self.b = ring % 2
        self.turn = turn


def pipelined(eng, n, unroll, lead, depth, step, before_loop=None):
    def peeled(i):
        def tile_of(skew):
            return Tile(i - skew, (i - skew) % 4, i // unroll) if 0 <= i - skew < n else None
        step(tile_of)

    def looped(r, k):
        def tile_of(skew):
            return Tile(r * unroll + (k - skew), (k - skew) % unroll if unroll == 4 else (k - skew) % 2, r)
        step(tile_of)

    assert lead % unroll == 0 and n % unroll == 0
    for i in range(lead):
        peeled(i)
    if before_loop is not None:
        before_loop()
    with eng.Fori(lead // unroll, n // unroll) as r:
        for k in range(unroll):
            looped(r, k)
    for i in range(n, n + depth):
        peeled(i)


def wait(eng, sem, count, most=None):
    if isinstance(count, int):
        if count <= 0:
            return
        if most is not None:
            count = min(count, most)
    eng.wait_ge(sem, count)


def wait_at_ends(eng, sem, count, most=None):
    if isinstance(count, int):
        wait(eng, sem, count, most)


def build(nc, X, Wq, Wv, q_norm_w, v_norm_w, Wg, W1, W2, W3, Ws1, Ws2, Ws3, out):
    B, L, D = X.shape
    H, d = q_norm_w.shape
    E = Wg.shape[1]
    F = W1.shape[2]
    FS = Ws1.shape[1]
    T = B * L
    NT = T // P
    NTB = L // P
    KC = D // P
    FC = FS // P
    PAIRS = T * TOP_K
    CAP = CAP_FACTOR * PAIRS // E
    NBE = T // P
    NB = E * NBE
    NJ = PAIRS // P + E
    HG = P // d
    NP_ = H // 2
    TG = 512
    NG = T // TG
    assert D == 256 and d == 16 and F == 128 and FS == 256 and E == 32

    ctx = ExitStack()
    with ctx:
        def sb(name, shape, dt=F32):
            return ctx.enter_context(nc.sbuf_tensor(name, shape, dt))

        def pb(name):
            return ctx.enter_context(nc.psum_tensor(name, [P, 512], F32))

        def sem(name):
            return ctx.enter_context(nc.semaphore(name))

        xn2_rows = nc.dram_tensor("xn2_rows", [T, D], F32).ap()
        lists = nc.dram_tensor("lists", [(NB + 1) * P, 1], F32).ap()
        y_rows = nc.dram_tensor("y_rows", [NJ * P, D], F32).ap()
        lists_blocks = lists.rearrange("(b r) o -> b (r o)", r=P)

        x_tiles = X.rearrange("b (t p) c -> p (b t) c", p=P)
        out_tiles = out.rearrange("b (t p) c -> (b t) p c", p=P)

        xall = sb("xall", [P, NT, D])
        x2T_all = sb("x2T_all", [P, KC, T])
        w13 = sb("w13", [P, E, KC, 2, F])
        w2 = sb("w2", [P, E, D])
        ws13 = sb("ws13", [P, KC, 2, FS])
        ws2 = sb("ws2", [P, FC, D])
        ident = sb("ident", [P, P])
        tri = sb("tri", [P, P])
        keep = sb("keep", [P, NT + 2])
        wqc = sb("wqc", [P, KC])
        wvc = sb("wvc", [P, KC])
        wg = sb("wg", [P, KC, E])
        par_i = sb("par_i", [P, 1], I32)
        par_f = sb("par_f", [P, 2])
        mwq = sb("mwq", [P, 2, KC])
        head_mask = sb("head_mask", [P, KC, P])
        tri_bf = sb("tri_bf", [P, P], BF16)
        ones_bf = sb("ones_bf", [P, P], BF16)
        eidx_i = sb("eidx_i", [P, NJ // 4], I32)
        eidx = sb("eidx", [P, NJ // 4])
        ebase = sb("ebase", [P, E])
        pair_i = sb("pair_i", [P, NT * TOP_K], I32)
        pair_all = sb("pair_all", [P, NT, TOP_K])

        st = sb("st", [P, 6])
        mv1 = sb("mv1", [P, 2, 2])
        rs1 = sb("rs1", [P, 2])
        st2 = sb("st2", [P, 6])
        mv2 = sb("mv2", [P, 2, 2])
        rs2 = sb("rs2", [P, 2])
        ss = sb("ss", [P, 2, 2 * H])
        rr = sb("rr", [P, 2, 2 * H])
        var1 = sb("var1", [P, 1])
        var2 = sb("var2", [P, 1])
        minus_half = sb("minus_half", [P, 1])
        eps_col = sb("eps_col", [P, 1])
        lnm = sb("lnm", [P, 2 * H])
        guess = sb("guess", [P, 2 * H])
        msq = sb("msq", [P, 2 * H])
        gg = sb("gg", [P, 2 * H])
        mgg = sb("mgg", [P, 2 * H])
        fac = sb("fac", [P, 2 * H])
        w_raw = sb("w_raw", [P, KC * P])
        w_bd = sb("w_bd", [P, 2, KC * P])
        lg = sb("lg", [P, 2, E])
        m8 = sb("m8", [P, 8])
        nmx = sb("nmx", [P, 2])
        ex = sb("ex", [P, 2, E])
        se = sb("se", [P, 2])
        rin = sb("rin", [P, 1])
        prob = sb("prob", [P, E])
        t8 = sb("t8", [P, 8])
        ix = sb("ix", [P, 8], U32)
        ixf = sb("ixf", [P, TOP_K])
        oh = sb("oh", [P, TOP_K, E])
        ohr = sb("ohr", [P, TOP_K, E])
        mask = sb("mask", [P, 2, E], BF16)
        mcum = sb("mcum", [P, 2, E], BF16)
        rk = sb("rk", [P, E])
        place = sb("place", [P, E])
        pos = sb("pos", [P, TOP_K])
        posi = sb("posi", [P, 2, TOP_K], I32)
        pid = sb("pid", [P, 2, TOP_K])
        posi_all = sb("posi_all", [P, NT, TOP_K], I32)
        wts = sb("wts", [P, NT, TOP_K])

        arena = w2[:].rearrange("p e c -> p (e c)")
        cut = [0]

        def part(width):
            cut[0] += width
            assert cut[0] <= E * D
            return arena[:, cut[0] - width:cut[0]]

        s_sb = part(2048).rearrange("p (j g r l) -> p j g r l", j=4, g=2, r=2)
        sq = part(512)
        qm = part(512).rearrange("p (r g l) -> p r g l", r=2, g=2)
        qn = part(512).rearrange("p (b c) -> p b c", b=2)
        qT = part(256).rearrange("p (g l) -> p g l", g=2)
        vp = part(2 * NP_ * 3 * d).rearrange("p (b n k e) -> p b n k e", b=2, n=NP_, k=3)
        xn = part(512).rearrange("p (b c) -> p b c", b=2)
        xnT = part(512).rearrange("p (b g m) -> p b g m", b=2, g=2)
        oT = part(512).rearrange("p (b g l) -> p b g l", b=2, g=2)
        xn2 = part(512).rearrange("p (b c) -> p b c", b=2)
        x2T = part(512).rearrange("p (b g l) -> p b g l", b=2, g=2)
        wqv = part(KC * 512).rearrange("p (k c) -> p k c", k=KC)
        wq_in = s_sb.rearrange("p j g r l -> p (j g r l)")[:, 0:512].rearrange("p (k c) -> p k c", k=2)
        wv_in = s_sb.rearrange("p j g r l -> p (j g r l)")[:, 512:1024].rearrange("p (k c) -> p k c", k=2)

        sg = sb("sg", [P, FC, TG])
        gsh = sb("gsh", [P, 2, FC, TG])
        pad = gsh[:].rearrange("p b f t -> p (b f t)")[:, 0:NB + 1]
        xg = sb("xg", [P, 4, D])
        after_a = gsh[:].rearrange("p b f t -> p (b f t)")
        xgT = after_a[:, 0:512].rearrange("p (b g m) -> p b g m", b=2, g=KC)
        sge = after_a[:, 512:768].rearrange("p (b f) -> p b f", b=2)
        ge = after_a[:, 768:1024].rearrange("p (b f) -> p b f", b=2)
        geT = after_a[:, 1024:1280].rearrange("p (b f) -> p b f", b=2)
        y = sg[:].rearrange("p f t -> p (f t)").rearrange("p (b c) -> p b c", b=4)
        rows = w13[:, 0:8].rearrange("p e k n f -> p (e k n f)").rearrange("p (b k c) -> p b k c", b=4, k=TOP_K)
        place_e = sb("place_e", [P, NT * TOP_K], I32)
        place_ef = sb("place_ef", [P, NT * TOP_K])
        shift = sb("shift", [P, NJ // 4])
        moved = sb("moved", [P, NT * TOP_K])
        rowf = sb("rowf", [P, NT * TOP_K])
        row_i = sb("row_i", [P, NT, TOP_K], I32)
        row_b = sb("row_b", [P, 4, TOP_K], I32)
        cnt_i = sb("cnt_i", [P, E], I32)
        nt_i = sb("nt_i", [P, E], I32)
        ntf = sb("ntf", [P, E])
        ones_f = sb("ones_f", [P, E])
        endt = sb("endt", [P, E])
        jc_i = sb("jc_i", [P, 2], I32)
        jc = sb("jc", [P, 2])
        behind = sb("behind", [P, 2, E])
        ej = sb("ej", [P, 2])
        bnt = sb("bnt", [P, 2, E])
        stj = sb("stj", [P, 2])
        jrel = sb("jrel", [P, 2])
        blk = sb("blk", [P, 2])
        blk_i = sb("blk_i", [P, 2], I32)
        ejc = sb("ejc", [P, 2])
        erow = sb("erow", [1, 256], I32)
        lj = sb("lj", [P, 2, P])
        slot_i = sb("slot_i", [P, NJ], I32)
        tok_i = sb("tok_i", [P, NJ], I32)
        tok_b = sb("tok_b", [P, 4], I32)
        rank_i = sb("rank_i", [P, NT * TOP_K], I32)
        inside = sb("inside", [P, NT * TOP_K])

        pT0, pT1, pQV, pO = pb("pT0"), pb("pT1"), pb("pQV"), pb("pO")
        pS = [pb(f"pS{j}") for j in range(4)]

        names = """var1_done var2_done ln_done guess_done msq_done gg_done mgg_done fac_done x_first x_rest w_in wc_in wg_in consts_pool consts_dve wt_ps wt_done
            stats1 mean1 rstd1 xn_done xnT_ps xnT_done qv_ps sq_done ss_done rms_done qn_done v_done
            qT_ps qm_done qT_done scores_ps masked state_ps raw_done state_done o_ps oT_done
            ot_ps x2_done stats2 mean2 rstd2 xn2_done x2T_ps x2T_done logits_ps
            lg_done max_done nmx_done exp_done rin_done prob_done top_done ix_done ixf_done oh_done mask_done
            mcum_done rank_ps place_done placed_done pos_done pos_kept pid_done lists_padded
            w13_in w2_in ws_in h_ps silu_done gsh_done z_ps z_done
            cnt_ps tabs tab_blk tab_lj_in tab_ps tab_done erow_ps erow_done added
            bcopy xT_ps xT_done hb_ps sge_done ge_done gT_ps gT_done y_ps y_done row_tab rcopy summed moved_done s_copied masked_pool rk_done""".split()
        S = {n: sem(n) for n in names}
        stored = [sem(f"stored{b}") for b in range(2)]
        scattered = [sem(f"scattered{b}") for b in range(2)]
        gathered = [sem(f"gathered{b}") for b in range(4)]
        put = [sem(f"put{b}") for b in range(4)]
        rows_in = [sem(f"rows_in{b}") for b in range(4)]
        passed = {e.engine: sem(n) for n, e in (("passed_pool", nc.gpsimd), ("passed_vector", nc.vector))}
        final = [sem(f"final{b}") for b in range(2)]
        lead_a, lead_b = 8, 12
        POOL_CONSTS = 27

        def settled(eng, sem, count):
            wait(eng, sem, count)
            if not isinstance(count, int):
                eng.sem_inc(passed[eng.engine], 1)

        block = ctx.enter_context(nc.Block())

        @block.sync
        def _(sp):
            sp.dma_start(xall[:, 0:lead_a, :], x_tiles[:, 0:lead_a, :]).then_inc(S["x_first"], 16)
            sp.dma_start(wq_in, Wq.rearrange("(k p) c -> p k c", p=P)).then_inc(S["w_in"], 16)
            sp.dma_start(wv_in, Wv.rearrange("(k p) c -> p k c", p=P)).then_inc(S["w_in"], 16)
            for wc, w in ((wqc, q_norm_w), (wvc, v_norm_w)):
                for g in range(KC):
                    sp.dma_start(wc[:, g:g + 1], w[g * HG:(g + 1) * HG, :].rearrange("h e -> (h e)").unsqueeze(1)
                                 ).then_inc(S["wc_in"], 16)
            sp.dma_start(wg[:], Wg.rearrange("(k p) e -> p k e", p=P)).then_inc(S["wg_in"], 16)
            sp.dma_start(xall[:, lead_a:NT, :], x_tiles[:, lead_a:NT, :]).then_inc(S["x_rest"], 16)
            sp.wait_ge(S["consts_pool"], 1)
            sp.dma_start(lists.rearrange("(p b) o -> p (b o)", p=P), pad).then_inc(S["lists_padded"], 16)
            for n, w in enumerate((Ws1, Ws3)):
                sp.dma_start(ws13[:, :, n, :], w.rearrange("(k p) f -> p k f", p=P)).then_inc(S["ws_in"], 16)
            sp.dma_start(ws2[:], Ws2.rearrange("(k p) c -> p k c", p=P)).then_inc(S["ws_in"], 16)
            for n, w in enumerate((W1, W3)):
                for k in range(KC):
                    sp.dma_start(w13[:, :, k, n, :], w[:, k * P:(k + 1) * P, :].rearrange("e p f -> p e f")
                                 ).then_inc(S["w13_in"], 16)

            def step(tile_of):
                if (a := tile_of(3)) is not None:
                    wait(sp, S["xn2_done"], a.t + 1)
                    sp.dma_start(xn2_rows.rearrange("(t p) c -> t p c", p=P)[bass.ds(a.t, 1)].rearrange("a p c -> (a p) c"),
                                 xn2[:, a.b, :]).then_inc(stored[a.b], 16)
            pipelined(sp, NT, 2, lead_a, 5, step)
            sp.wait_ge(S["o_ps"], NT)
            sp.wait_ge(S["ot_ps"], NT)
            sp.wait_ge(S["logits_ps"], NT)
            for b in range(2):
                sp.wait_ge(stored[b], 16 * NT // 2)
            sp.dma_start(w2[:], W2.rearrange("e p c -> p e c")).then_inc(S["w2_in"], 16)

            def store_step(tile_of):
                if (a := tile_of(7)) is not None:
                    wait(sp, S["y_done"], a.t + 1)
                    sp.dma_start(y_rows.rearrange("(t p) c -> t p c", p=P)[bass.ds(a.t, 1)].rearrange("a p c -> (a p) c"),
                                 y[:, a.ring, :]).then_inc(put[a.ring], 16)
            pipelined(sp, NJ, 4, lead_b, 8, store_step)

            def out_step(tile_of):
                if (a := tile_of(0)) is not None:
                    wait(sp, S["summed"], a.t + 1)
                    sp.dma_start(out_tiles[bass.ds(a.t, 1)].rearrange("a p c -> (a p) c"),
                                 xall[:, bass.ds(a.t, 1), :].rearrange("p a c -> p (a c)")).then_inc(final[a.b], 16)
            pipelined(sp, NT, 2, 2, 0, out_step)
            for b in range(2):
                sp.wait_ge(final[b], 16 * NT // 2)

        @block.gpsimd
        def _(pool):
            def pool_wait(sem, count):
                settled(pool, sem, count)

            pool.memset(pad, float(PAIRS)).then_inc(S["consts_pool"], 1)
            c = [1]

            def chain(ins):
                c[0] += 1
                ins.then_inc(S["consts_pool"], 1)
                pool.wait_ge(S["consts_pool"], c[0])

            chain(pool.memset(ident[:], 0.0))
            chain(pool.affine_select(out=ident[:], in_=ident[:], compare_op=ALU.not_equal, fill=1.0, base=0,
                                     pattern=[[-1, P]], channel_multiplier=1))
            chain(pool.memset(tri[:], 1.0))
            chain(pool.affine_select(out=tri[:], in_=tri[:], compare_op=ALU.is_ge, fill=0.0, base=0,
                                     pattern=[[1, P]], channel_multiplier=-1))
            chain(pool.memset(tri_bf[:], 1.0))
            chain(pool.affine_select(out=tri_bf[:], in_=tri_bf[:], compare_op=ALU.is_ge, fill=0.0, base=-1,
                                     pattern=[[1, P]], channel_multiplier=-1))
            chain(pool.memset(ones_bf[:], 1.0))
            chain(pool.memset(ones_f[:], 1.0))
            chain(pool.memset(head_mask[:], 1.0))
            for base, mult in ((0, 1), (d - 1, -1)):
                for g in range(KC):
                    v = head_mask[:, g, :].rearrange("p (h e) -> p h e", e=d)
                    chain(pool.affine_select(out=v, in_=v, compare_op=ALU.is_ge, fill=0.0, base=base,
                                             pattern=[[-d * mult, HG], [0, d]], channel_multiplier=mult))
            chain(pool.iota(par_i[:], pattern=[[0, 1]], base=0, channel_multiplier=1))
            chain(pool.iota(eidx_i[:], pattern=[[1, NJ // 4]], base=0, channel_multiplier=0))
            chain(pool.iota(pair_i[:], pattern=[[P * TOP_K, NT], [1, TOP_K]], base=0, channel_multiplier=TOP_K))
            chain(pool.iota(jc_i[:], pattern=[[P, 2]], base=0, channel_multiplier=1))
            chain(pool.memset(keep[:], 1.0))
            for s in range(B):
                chain(pool.memset(keep[:, s * NTB:s * NTB + 1], 0.0))
            chain(pool.memset(w_raw[:], 0.0))
            chain(pool.memset(w_bd[:], 0.0))
            chain(pool.memset(vp, 0.0))
            chain(pool.memset(mcum[:], 0.0))
            chain(pool.memset(minus_half[:], -0.5))
            chain(pool.memset(eps_col[:], RMS_EPS))
            assert c[0] == POOL_CONSTS
            pool.wait_ge(S["consts_dve"], 5)
            pool.wait_ge(S["lists_padded"], 16)

            def scatter(a, k):
                pool.indirect_dma_start(out=lists, out_offset=bass.IndirectOffsetOnAxis(ap=posi[:, a.b, k:k + 1], axis=0),
                                        in_=pid[:, a.b, k:k + 1], in_offset=None).then_inc(scattered[a.b], 16)

            def step(tile_of):
                if (a := tile_of(0)) is not None:
                    pool_wait(S["mean1"], a.t + 1)
                    pool_wait(S["xn_done"], a.t - 1)
                    pool.tensor_scalar(var1[:], mv1[:, a.b, 1:2], LN_EPS, None, ALU.add).then_inc(S["var1_done"], 1)
                    pool_wait(S["var1_done"], a.t + 1)
                    pool.tensor_tensor(rs1[:, a.b:a.b + 1], var1[:], minus_half[:], ALU.pow
                                       ).then_inc(S["rstd1"], 1)
                if (a := tile_of(6)) is not None:
                    pool_wait(scattered[a.b], (a.t - a.b) * 32)
                    pool.tensor_copy(pid[:, a.b, :], pair_all[:, bass.ds(a.t, 1), :].rearrange("p a k -> p (a k)")
                                     ).then_inc(S["pid_done"], 1)
                    pool_wait(S["pid_done"], a.t + 1)
                    pool_wait(S["pos_done"], a.t + 1)
                    scatter(a, 0)
                    scatter(a, 1)
                if (a := tile_of(4)) is not None:
                    pool_wait(S["mean2"], a.t + 1)
                    pool_wait(S["xn2_done"], a.t - 1)
                    pool.tensor_scalar(var2[:], mv2[:, a.b, 1:2], LN_EPS, None, ALU.add).then_inc(S["var2_done"], 1)
                    pool_wait(S["var2_done"], a.t + 1)
                    pool.tensor_tensor(rs2[:, a.b:a.b + 1], var2[:], minus_half[:], ALU.pow
                                       ).then_inc(S["rstd2"], 1)
                if (a := tile_of(1)) is not None:
                    pool_wait(S["guess_done"], a.t + 1)
                    pool_wait(S["v_done"], a.t - 1)
                    pool.tensor_scalar(msq[:], ss[:, a.b, :], RMS_EPS, None, ALU.add).then_inc(S["msq_done"], 1)
                    pool.tensor_tensor(gg[:], guess[:], guess[:], ALU.mult).then_inc(S["gg_done"], 1)
                    pool_wait(S["msq_done"], a.t + 1)
                    pool_wait(S["gg_done"], a.t + 1)
                    pool.tensor_tensor(mgg[:], msq[:], gg[:], ALU.mult).then_inc(S["mgg_done"], 1)
                    pool_wait(S["mgg_done"], a.t + 1)
                    pool.tensor_scalar(fac[:], mgg[:], -0.5, 1.5, ALU.mult, ALU.add).then_inc(S["fac_done"], 1)
                    pool_wait(S["fac_done"], a.t + 1)
                    pool.tensor_tensor(rr[:, a.b, :], guess[:], fac[:], ALU.mult).then_inc(S["rms_done"], 1)
                if (a := tile_of(6)) is not None:
                    scatter(a, 2)
                    scatter(a, 3)
                if (a := tile_of(2)) is not None:
                    for j in range(2):
                        pool_wait(S["s_copied"], 2 * a.t + j + 1)
                        v = s_sb[:, j].rearrange("p g r l -> p (g r) l")
                        pool.affine_select(out=v, in_=v, compare_op=ALU.is_ge, fill=0.0, base=0,
                                           pattern=[[0, 4], [1, P]], channel_multiplier=-1).then_inc(S["masked_pool"], 1)
            pipelined(pool, NT, 2, lead_a, 6, step)

            pool.wait_ge(S["tab_blk"], 1)
            for b in range(2):
                pool.wait_ge(scattered[b], 64 * NT // 2)
            for n, rows_n in enumerate((P, NJ - P)):
                pool.indirect_dma_start(out=lj[0:rows_n, n, :], out_offset=None, in_=lists_blocks,
                                        in_offset=bass.IndirectOffsetOnAxis(ap=blk_i[0:rows_n, n:n + 1], axis=0)
                                        ).then_inc(S["tab_lj_in"], 16)
            pool.wait_ge(S["tab_done"], 1)

            def expert_step(tile_of):
                if (a := tile_of(1)) is not None:
                    pool_wait(S["xT_ps"], a.t - 3)
                    pool_wait(S["bcopy"], a.t + 1)
                    pool.indirect_dma_start(out=xg[:, a.ring, :], out_offset=None, in_=xn2_rows,
                                            in_offset=bass.IndirectOffsetOnAxis(ap=tok_b[:, a.ring:a.ring + 1], axis=0)
                                            ).then_inc(gathered[a.ring], 16)
            pipelined(pool, NJ, 4, lead_b, 8, expert_step)

            for b in range(4):
                pool.wait_ge(put[b], 16 * NJ // 4)
            pool.wait_ge(S["hb_ps"], NJ)

            def rows_step(tile_of):
                if (a := tile_of(0)) is not None:
                    pool_wait(S["summed"], a.t - 3)
                    pool_wait(S["rcopy"], a.t + 1)
                    for k in range(TOP_K):
                        pool.indirect_dma_start(out=rows[:, a.ring, k, :], out_offset=None, in_=y_rows,
                                                in_offset=bass.IndirectOffsetOnAxis(ap=row_b[:, a.ring, k:k + 1], axis=0)
                                                ).then_inc(rows_in[a.ring], 16)
            pipelined(pool, NT, 4, 4, 0, rows_step)

        @block.scalar
        def _(act):
            for k in range(KC):
                act.wait_ge(S["wt_ps"], k + 1)
                act.copy(wqv[:, k, :], (pT0, pT1)[k][:]).then_inc(S["wt_done"], 1)

            def copy_scores(a, j):
                wait(act, S["scores_ps"], 4 * a.t + j + 1)
                wait(act, S["o_ps"], a.t)
                act.copy(s_sb[:, j].rearrange("p g r l -> p (g r l)"), pS[j][:]).then_inc(S["s_copied"], 1)

            def step(tile_of):
                if (a := tile_of(5)) is not None:
                    wait(act, S["nmx_done"], a.t + 1)
                    wait(act, S["prob_done"], a.t - 1)
                    act.activation(ex[:, a.b, :], lg[:, a.b, :], ACT.Exp, bias=nmx[:, a.b:a.b + 1], scale=1.0,
                                   accum_out=se[:, a.b:a.b + 1]).then_inc(S["exp_done"], 1)
                if (a := tile_of(1)) is not None:
                    wait(act, S["qv_ps"], a.t + 1)
                    wait(act, S["ss_done"], a.t)
                    act.activation(sq, pQV[:], ACT.Square, scale=float(d) ** -0.5).then_inc(S["sq_done"], 1)
                if (a := tile_of(2)) is not None:
                    wait(act, S["qT_ps"], a.t + 1)
                    wait(act, S["scores_ps"], 4 * a.t)
                    for r in range(2):
                        for g in range(KC):
                            last = act.activation(qm[:, r, g, :], pT1[:, g * P:(g + 1) * P], ACT.Copy,
                                                  scale=mwq[:, r, g:g + 1])
                    last.then_inc(S["qm_done"], 1)
                if (a := tile_of(1)) is not None:
                    wait(act, S["ss_done"], a.t + 1)
                    act.activation(lnm[:], ss[:, a.b, :], ACT.Ln, bias=eps_col[:]).then_inc(S["ln_done"], 1)
                    wait(act, S["ln_done"], a.t + 1)
                    wait(act, S["rms_done"], a.t)
                    act.activation(guess[:], lnm[:], ACT.Exp, scale=-0.5).then_inc(S["guess_done"], 1)
                if (a := tile_of(3)) is not None:
                    wait(act, S["o_ps"], a.t + 1)
                    wait(act, S["ot_ps"], a.t - 1)
                    for g in range(KC):
                        last = act.activation(oT[:, a.b, g, :], pO[:, g * P:(g + 1) * P], ACT.Copy, scale=wvc[:, g:g + 1])
                    last.then_inc(S["oT_done"], 1)
                if (a := tile_of(2)) is not None:
                    wait(act, S["o_ps"], a.t)
                    act.copy(qT, pT1[:, 0:D].rearrange("p (g m) -> p g m", g=KC)).then_inc(S["qT_done"], 1)
                if (a := tile_of(4)) is not None:
                    wait(act, S["x2T_ps"], a.t + 1)
                    wait(act, S["logits_ps"], a.t - 1)
                    src = pT0[:, 0:D].rearrange("p (g m) -> p g m", g=KC)
                    act.copy(x2T[:, a.b], src)
                    act.copy(x2T_all[:].rearrange("p k (t l) -> p k t l", l=P)[:, :, bass.ds(a.t, 1), :].rearrange("p k a l -> p k (a l)"),
                             src).then_inc(S["x2T_done"], 1)
                if (a := tile_of(2)) is not None:
                    copy_scores(a, 0)
                if (a := tile_of(0)) is not None:
                    wait(act, S["xnT_ps"], a.t + 1)
                    wait(act, S["qv_ps"], a.t - 1)
                    wait(act, S["scores_ps"], 4 * (a.t - 1))
                    act.copy(xnT[:, a.b], pT0[:, 0:D].rearrange("p (g m) -> p g m", g=KC)).then_inc(S["xnT_done"], 1)
                if (a := tile_of(2)) is not None:
                    copy_scores(a, 1)
                if (a := tile_of(5)) is not None:
                    wait(act, S["rank_ps"], a.t + 1)
                    wait(act, S["placed_done"], a.t)
                    act.copy(rk[:], pT1[:, 0:E]).then_inc(S["rk_done"], 1)
                if (a := tile_of(4)) is not None:
                    wait(act, S["logits_ps"], a.t + 1)
                    wait(act, S["nmx_done"], a.t - 1)
                    wait(act, S["exp_done"], a.t - 1)
                    act.copy(lg[:, a.b, :], pO[:, 0:E]).then_inc(S["lg_done"], 1)
            act.wait_ge(S["wc_in"], 64)
            act.wait_ge(S["consts_pool"], POOL_CONSTS)
            act.wait_ge(S["consts_dve"], 8)
            act.preload_act_table_set("natural_log_exp_and_others")
            pipelined(act, NT, 2, lead_a, 6, step)

            act.preload_act_table(ACT.Silu)

            def expert_step(tile_of):
                if (a := tile_of(4)) is not None:
                    wait(act, S["xT_ps"], a.t + 1)
                    wait(act, S["hb_ps"], a.t - 1)
                    act.copy(xgT[:, a.b], pT0[:, 0:D].rearrange("p (g m) -> p g m", g=KC)).then_inc(S["xT_done"], 1)
                if (a := tile_of(5)) is not None:
                    wait(act, S["hb_ps"], a.t + 1)
                    wait(act, S["ge_done"], a.t - 1)
                    act.activation(sge[:, a.b, :], pS[a.b][:, 0:F], ACT.Silu).then_inc(S["sge_done"], 1)
                if (a := tile_of(7)) is not None:
                    wait(act, S["y_ps"], a.t + 1)
                    wait(act, put[a.ring], (a.t - a.ring) * 4)
                    act.copy(y[:, a.ring, :], pS[2 + a.b][:, 0:D]).then_inc(S["y_done"], 1)
            pipelined(act, NJ, 4, lead_b, 8, expert_step)
            for b in range(4):
                act.wait_ge(put[b], 16 * NJ // 4)

            def shared_step(tile_of):
                if (a := tile_of(0)) is not None:
                    for m in range(FC):
                        wait(act, S["h_ps"], FC * a.t + m + 1)
                        wait(act, S["gsh_done"], FC * (a.t - 1) + m + 1)
                        act.activation(sg[:, m, :], pS[2 * m][:], ACT.Silu).then_inc(S["silu_done"], 1)
            pipelined(act, NG, 2, 2, 1, shared_step)

        @block.tensor
        def _(pe):
            pe.wait_ge(S["w_in"], 32)
            pe.wait_ge(S["consts_pool"], POOL_CONSTS)
            for k in range(KC):
                for n, w in enumerate((wq_in, wv_in)):
                    for o in range(KC):
                        at = n * D + o * P
                        last = pe.transpose((pT0, pT1)[k][:, at:at + P], w[:, o, k * P:(k + 1) * P], ident[:])
                last.then_inc(S["wt_ps"], 1)
            pe.wait_ge(S["wt_done"], KC)
            pe.wait_ge(S["consts_dve"], 5)
            pe.wait_ge(S["wg_in"], 16)

            def step(tile_of):
                if (a := tile_of(1)) is not None:
                    wait(pe, S["xnT_done"], a.t + 1)
                    wait(pe, S["v_done"], a.t)
                    for k in range(KC):
                        last = pe.matmul(pQV[:], xnT[:, a.b, k, :], wqv[:, k, :], start=(k == 0), stop=(k == KC - 1))
                    last.then_inc(S["qv_ps"], 1)
                if (a := tile_of(4)) is not None:
                    wait(pe, S["oT_done"], a.t + 1)
                    wait(pe, S["masked"], 2 * a.t + 4, 2 * NT)
                    wait_at_ends(pe, S["x2_done"], a.t)
                    for g in range(KC):
                        last = pe.transpose(pS[3][:, g * P:(g + 1) * P], oT[:, a.b, g, :], ident[:])
                    last.then_inc(S["ot_ps"], 1)
                if (a := tile_of(2)) is not None:
                    wait(pe, S["qn_done"], a.t + 1)
                    wait(pe, S["rk_done"], a.t - 3)
                    wait(pe, S["qT_done"], a.t)
                    for g in range(KC):
                        last = pe.transpose(pT1[:, g * P:(g + 1) * P], qn[:, a.b, g * P:(g + 1) * P], ident[:])
                    last.then_inc(S["qT_ps"], 1)
                if (a := tile_of(3)) is not None:
                    wait(pe, S["qT_done"], a.t + 1)
                    wait(pe, S["state_done"], a.t)
                    wait(pe, S["lg_done"], a.t - 1)
                    wait_at_ends(pe, S["oT_done"], a.t)
                    wait(pe, S["masked"], 2 * a.t + 2)
                    wait(pe, S["masked_pool"], 2 * a.t + 2)
                    for g in range(KC):
                        pe.matmul(pO[:, g * P:(g + 1) * P], w_bd[:, a.b, g * P:(g + 1) * P], qT[:, g, :],
                                  start=(g == 0), stop=False, skip_group_check=True)
                    for g in range(KC):
                        for r in range(2):
                            for j in range(4):
                                last = pe.matmul(pO[32 * j:32 * j + 32, g * P:(g + 1) * P],
                                                 vp[:, a.b, 4 * g + j, r:r + 2, :], s_sb[:, j, g, r, :],
                                                 start=False, stop=(r == 1), skip_group_check=True)
                    last.then_inc(S["o_ps"], 1)
                if (a := tile_of(2)) is not None:
                    wait(pe, S["v_done"], a.t + 1)
                    wait_at_ends(pe, S["raw_done"], a.t)
                    wait_at_ends(pe, S["x2T_done"], a.t - 2)
                    for g in range(KC):
                        last = pe.matmul(pT0[:, g * P:(g + 1) * P], xn[:, a.b, g * P:(g + 1) * P],
                                         vp[:, a.b, 4 * g:4 * g + 4, 0:3:2, :], start=True, stop=True)
                    last.then_inc(S["state_ps"], 1)
                    wait(pe, S["qm_done"], a.t + 1)
                    wait(pe, S["x2_done"], a.t - 1)
                    wait_at_ends(pe, S["masked"], 2 * a.t)
                    wait_at_ends(pe, S["s_copied"], 2 * a.t)
                for g, j in ((g, j) for g in range(KC) for j in range(4)):
                    if (a := tile_of(2)) is not None:
                        last = pe.matmul(pS[j][:, g * 256:(g + 1) * 256], xnT[32 * j:32 * j + 32, a.b, g, :],
                                         qm[32 * j:32 * j + 32, :, g, :], start=(g == 0), stop=True,
                                         skip_group_check=True)
                        if g == KC - 1:
                            last.then_inc(S["scores_ps"], 1)
                    if (g, j) == (KC - 1, 1) and (a := tile_of(4)) is not None:
                        wait(pe, S["xn2_done"], a.t + 1)
                        wait(pe, S["raw_done"], a.t + 3, NT)
                        wait_at_ends(pe, S["x2T_done"], a.t)
                        for c in range(KC):
                            last = pe.transpose(pT0[:, c * P:(c + 1) * P], xn2[:, a.b, c * P:(c + 1) * P], ident[:])
                        last.then_inc(S["x2T_ps"], 1)
                if (a := tile_of(5)) is not None:
                    wait(pe, S["mask_done"], a.t + 1)
                    wait(pe, S["mcum_done"], a.t)
                    wait(pe, S["qT_done"], a.t + 4, NT)
                    wait_at_ends(pe, S["rk_done"], a.t)
                    pe.matmul(pT1[:, 0:E], tri_bf[:], mask[:, a.b, :], start=True, stop=False)
                    pe.matmul(pT1[:, 0:E], ones_bf[:], mcum[:, a.b, :], start=False, stop=True).then_inc(S["rank_ps"], 1)
                if (a := tile_of(0)) is not None:
                    wait(pe, S["xn_done"], a.t + 1)
                    wait(pe, S["x2T_done"], a.t - 3)
                    wait_at_ends(pe, S["raw_done"], a.t - 1)
                    for g in range(KC):
                        last = pe.transpose(pT0[:, g * P:(g + 1) * P], xn[:, a.b, g * P:(g + 1) * P], ident[:])
                    last.then_inc(S["xnT_ps"], 1)
                if (a := tile_of(4)) is not None:
                    wait(pe, S["x2T_done"], a.t + 1)
                    wait(pe, S["oT_done"], a.t + 2, NT)
                    wait_at_ends(pe, S["lg_done"], a.t)
                    for k in range(KC):
                        last = pe.matmul(pO[:, 0:E], x2T[:, a.b, k, :], wg[:, k, :], start=(k == 0), stop=(k == KC - 1))
                    last.then_inc(S["logits_ps"], 1)
            pipelined(pe, NT, 2, lead_a, 6, step)

            pe.wait_ge(S["mcum_done"], NT)
            pe.wait_ge(S["rk_done"], NT)
            pe.matmul(pT1[:, 0:E], ones_bf[:], mcum[:, NT % 2, :], start=True, stop=True).then_inc(S["cnt_ps"], 1)
            pe.wait_ge(S["tab_blk"], 1)
            for n in range(2):
                last = pe.matmul(pT1[0:1, n * P:(n + 1) * P], ejc[:, n:n + 1], ident[:], start=True, stop=True)
            last.then_inc(S["erow_ps"], 1)
            pe.wait_ge(S["tab_lj_in"], 32)
            pe.transpose(pT0[:, 0:P], lj[:, 0, :], ident[:])
            pe.transpose(pT0[:, P:NJ], lj[0:NJ - P, 1, :], ident[0:NJ - P, 0:NJ - P]).then_inc(S["tab_ps"], 1)
            pe.wait_ge(S["tab_done"], 1)
            pe.wait_ge(S["erow_done"], 1)
            pe.wait_ge(S["w13_in"], 16 * 2 * KC)
            pe.wait_ge(S["w2_in"], 16)
            pe.wait_ge(S["masked"], 2 * NT)

            number = [pe.alloc_register(f"expert{n}") for n in range(4)]

            def load_number(a):
                pe.reg_load(number[a.ring], erow[0:1, bass.ds(a.t, 1)])

            def expert_of(a):
                return nc.s_assert_within(pe.snap(number[a.ring]), 0, E - 1, skip_runtime_bounds_check_because="the table holds experts 0 .. E-1 only")

            def expert_step(tile_of):
                if (a := tile_of(4)) is not None:
                    wait(pe, gathered[a.ring], (a.t - a.ring) * 4 + 16)
                    wait(pe, S["xT_done"], a.t)
                    for g in range(KC):
                        last = pe.transpose(pT0[:, g * P:(g + 1) * P], xg[:, a.ring, g * P:(g + 1) * P], ident[:])
                    last.then_inc(S["xT_ps"], 1)
                if (a := tile_of(5)) is not None:
                    e = expert_of(a)
                    wait(pe, S["xT_done"], a.t + 1)
                    wait(pe, S["ge_done"], a.t - 1)
                    for k in range(KC):
                        last = pe.matmul(pS[a.b][:, 0:2 * F], xgT[:, a.b, k, :],
                                         w13[:, bass.ds(e, 1), k, :, :].rearrange("p a n f -> p (a n f)"),
                                         start=(k == 0), stop=(k == KC - 1))
                    last.then_inc(S["hb_ps"], 1)
                if (a := tile_of(4)) is not None:
                    load_number(a)
                if (a := tile_of(6)) is not None:
                    wait(pe, S["ge_done"], a.t + 1)
                    wait(pe, S["gT_done"], a.t)
                    pe.transpose(pT1[:, 0:P], ge[:, a.b, :], ident[:]).then_inc(S["gT_ps"], 1)
                if (a := tile_of(7)) is not None:
                    e = expert_of(a)
                    wait(pe, S["gT_done"], a.t + 1)
                    wait(pe, S["y_done"], a.t - 1)
                    pe.matmul(pS[2 + a.b][:, 0:D], geT[:, a.b, :],
                              w2[:, bass.ds(e, 1), :].rearrange("p a c -> p (a c)"), start=True, stop=True
                              ).then_inc(S["y_ps"], 1)
            pipelined(pe, NJ, 4, lead_b, 8, expert_step)
            pe.wait_ge(S["y_done"], NJ)

            pe.wait_ge(S["ws_in"], 48)

            def shared_step(tile_of):
                if (a := tile_of(0)) is not None:
                    for m in range(FC):
                        wait(pe, S["gsh_done"], FC * (a.t - 1) + m + 1)
                        for n in range(2):
                            for k in range(KC):
                                last = pe.matmul(pS[2 * m + n][:], ws13[:, k, n, m * P:(m + 1) * P],
                                                 x2T_all[:, k, bass.ds(a.t * TG, TG)], start=(k == 0), stop=(k == KC - 1))
                        last.then_inc(S["h_ps"], 1)
                if (a := tile_of(1)) is not None:
                    wait(pe, S["gsh_done"], FC * (a.t + 1))
                    for q in range(TG // P):
                        wait(pe, S["z_done"], 4 * a.t + q - 1)
                        for m in range(FC):
                            last = pe.matmul((pQV, pO)[q % 2][:, 0:D], gsh[:, a.b, m, q * P:(q + 1) * P], ws2[:, m, :],
                                             start=(m == 0), stop=(m == FC - 1))
                        last.then_inc(S["z_ps"], 1)
            pipelined(pe, NG, 2, 4, 1, shared_step)

        @block.vector
        def _(dve):
            dve.wait_ge(S["consts_pool"], POOL_CONSTS)
            dve.wait_ge(S["wc_in"], 64)
            c = [0]

            def chain(ins):
                c[0] += 1
                ins.then_inc(S["consts_dve"], 1)
                dve.wait_ge(S["consts_dve"], c[0])

            chain(dve.tensor_scalar(par_i[:], par_i[:], 4, 1, ALU.logical_shift_right, ALU.bitwise_and))
            chain(dve.tensor_copy(par_f[:, 1:2], par_i[:]))
            chain(dve.tensor_scalar(par_f[:, 0:1], par_f[:, 1:2], -1.0, 1.0, ALU.mult, ALU.add))
            chain(dve.tensor_copy(eidx[:], eidx_i[:]))
            chain(dve.tensor_copy(pair_all[:].rearrange("p t k -> p (t k)"), pair_i[:]))
            chain(dve.tensor_scalar(ebase[:], eidx[:, 0:E], float(T), None, ALU.mult))
            for r in range(2):
                chain(dve.tensor_scalar(mwq[:, r, :], wqc[:], par_f[:, r:r + 1], None, ALU.mult))
            for g in range(KC):
                chain(dve.tensor_scalar(head_mask[:, g, :], head_mask[:, g, :], wqc[:, g:g + 1], None, ALU.mult))
            chain(dve.tensor_copy(jc[:], jc_i[:]))

            def x_tile(a):
                return xall[:, bass.ds(a.t, 1), :].rearrange("p a c -> p (a c)")

            def step(tile_of):
                a0, a1, a2, a4, a5, a6 = (tile_of(s) for s in (0, 1, 2, 4, 5, 6))
                if a0 is not None:
                    dve.bn_stats(st[:], x_tile(a0)).then_inc(S["stats1"], 1)
                if a6 is not None:
                    wait(dve, S["rk_done"], a6.t + 1)
                    dve.tensor_tensor(place[:], rk[:], ebase[:], ALU.add).then_inc(S["placed_done"], 1)
                if a5 is not None:
                    settled(dve, S["lg_done"], a5.t + 1)
                    dve.max(m8[:], lg[:, a5.b, :]).then_inc(S["max_done"], 1)
                if a0 is not None:
                    settled(dve, S["stats1"], a0.t + 1)
                    dve.bn_aggr(mv1[:, a0.b, :], st[:]).then_inc(S["mean1"], 1)
                if a6 is not None:
                    wait(dve, S["placed_done"], a6.t + 1)
                    dve.tensor_tensor(ohr[:], oh[:], place[:].unsqueeze(1).to_broadcast([P, TOP_K, E]), ALU.mult
                                      ).then_inc(S["place_done"], 1)
                if a5 is not None:
                    wait(dve, S["max_done"], a5.t + 1)
                    wait(dve, S["exp_done"], a5.t - 1)
                    dve.tensor_scalar(nmx[:, a5.b:a5.b + 1], m8[:, 0:1], -1.0, None, ALU.mult).then_inc(S["nmx_done"], 1)
                if a6 is not None:
                    wait(dve, S["place_done"], a6.t + 1)
                    dve.tensor_reduce(pos[:], ohr[:], AX_X, ALU.add).then_inc(S["pos_kept"], 1)
                if a6 is not None:
                    wait(dve, S["pos_kept"], a6.t + 1)
                    wait(dve, scattered[a6.b], (a6.t - a6.b) * 32)
                    dve.tensor_copy(posi[:, a6.b, :], pos[:]).then_inc(S["pos_done"], 1)
                    dve.tensor_copy(posi_all[:, bass.ds(a6.t, 1), :].rearrange("p a k -> p (a k)"), pos[:])
                if a5 is not None:
                    t1 = a5.t + 1
                    wait(dve, S["exp_done"], t1)
                    dve.reciprocal(rin[:], se[:, a5.b:a5.b + 1]).then_inc(S["rin_done"], 1)
                if a4 is not None:
                    wait(dve, S["ot_ps"], a4.t + 1)
                    dve.tensor_tensor(x_tile(a4), x_tile(a4), pS[3][:, 0:D], ALU.add).then_inc(S["x2_done"], 1)
                if a5 is not None:
                    wait(dve, S["rin_done"], t1)
                    dve.tensor_scalar(prob[:], ex[:, a5.b, :], rin[:], None, ALU.mult).then_inc(S["prob_done"], 1)
                if a4 is not None:
                    settled(dve, S["x2_done"], a4.t + 1)
                    dve.bn_stats(st2[:], x_tile(a4)).then_inc(S["stats2"], 1)
                if a1 is not None:
                    wait(dve, S["sq_done"], a1.t + 1)
                    wait(dve, S["rms_done"], a1.t - 1)
                    dve.tensor_reduce(ss[:, a1.b, :], sq.rearrange("p (h e) -> p h e", e=d), AX_X, ALU.add
                                      ).then_inc(S["ss_done"], 1)
                if a5 is not None:
                    settled(dve, S["prob_done"], t1)
                    dve.max(t8[:], prob[:]).then_inc(S["top_done"], 1)
                if a4 is not None:
                    settled(dve, S["stats2"], a4.t + 1)
                    dve.bn_aggr(mv2[:, a4.b, :], st2[:]).then_inc(S["mean2"], 1)
                if a5 is not None:
                    settled(dve, S["top_done"], t1)
                    dve.max_index(ix[:], t8[:], prob[:]).then_inc(S["ix_done"], 1)
                    dve.tensor_copy(wts[:, bass.ds(a5.t, 1), :].rearrange("p a k -> p (a k)"), t8[:, 0:TOP_K])
                if a5 is not None:
                    wait(dve, S["ix_done"], t1)
                    dve.tensor_copy(ixf[:], ix[:, 0:TOP_K]).then_inc(S["ixf_done"], 1)
                if a2 is not None:
                    wait(dve, S["state_ps"], a2.t + 1)
                    dve.scalar_tensor_tensor(out=w_raw[:], in0=w_raw[:], scalar=keep[:, bass.ds(a2.t, 1)], in1=pT0[:, 0:D],
                                             op0=ALU.mult, op1=ALU.add).then_inc(S["raw_done"], 1)
                if a5 is not None:
                    wait(dve, S["ixf_done"], t1)
                    dve.tensor_tensor(oh[:], eidx[:, 0:E].unsqueeze(1).to_broadcast([P, TOP_K, E]),
                                      ixf[:].unsqueeze(2).to_broadcast([P, TOP_K, E]), ALU.is_equal).then_inc(S["oh_done"], 1)
                if a2 is not None:
                    wait(dve, S["raw_done"], a2.t + 1)
                    wait(dve, S["o_ps"], a2.t)
                    dve.scalar_tensor_tensor(out=w_bd[:, 1 - a2.b, :], in0=w_raw[:], scalar=keep[:, bass.ds(a2.t + 1, 1)],
                                             in1=head_mask[:].rearrange("p g c -> p (g c)"), op0=ALU.mult, op1=ALU.mult
                                             ).then_inc(S["state_done"], 1)
                if a5 is not None:
                    wait(dve, S["oh_done"], t1)
                    with nc.allow_low_precision("0 and 1 are exact"):
                        dve.tensor_reduce(mask[:, a5.b, :], oh[:].rearrange("p k e -> p e k"), AX_X, ALU.add
                                          ).then_inc(S["mask_done"], 1)
                if a0 is not None:
                    wait(dve, S["rstd1"], a0.t + 1)
                    wait(dve, S["state_ps"], a0.t - 1)
                    dve.tensor_scalar(xn[:, a0.b, :], x_tile(a0), mv1[:, a0.b, 0:1], rs1[:, a0.b:a0.b + 1],
                                      ALU.subtract, ALU.mult).then_inc(S["xn_done"], 1)
                if a4 is not None:
                    wait(dve, S["rstd2"], a4.t + 1)
                    wait(dve, S["x2T_ps"], a4.t - 1)
                    wait(dve, stored[a4.b], (a4.t - a4.b) * 8)
                    dve.tensor_scalar(xn2[:, a4.b, :], x_tile(a4), mv2[:, a4.b, 0:1], rs2[:, a4.b:a4.b + 1],
                                      ALU.subtract, ALU.mult).then_inc(S["xn2_done"], 1)
                if a5 is not None:
                    wait(dve, S["mask_done"], t1)
                    wait(dve, S["rank_ps"], a5.t)
                    dve.tensor_tensor(mcum[:, 1 - a5.b, :], mcum[:, a5.b, :], mask[:, a5.b, :], ALU.add
                                      ).then_inc(S["mcum_done"], 1)
                if a1 is not None:
                    wait(dve, S["rms_done"], a1.t + 1)
                    wait(dve, S["qT_ps"], a1.t - 1)
                    dve.tensor_tensor(qn[:, a1.b, :].rearrange("p (h e) -> p h e", e=d), pQV[:, 0:D].rearrange("p (h e) -> p h e", e=d),
                                      rr[:, a1.b, 0:H].unsqueeze(2).to_broadcast([P, H, d]), ALU.mult).then_inc(S["qn_done"], 1)
                    wait(dve, S["o_ps"], a1.t - 1)
                    dve.tensor_tensor(vp[:, a1.b, :, 0:3:2, :], pQV[:, D:2 * D].rearrange("p (n r e) -> p n r e", r=2, e=d),
                                      rr[:, a1.b, H:2 * H].rearrange("p (n r) -> p n r", r=2).unsqueeze(3).to_broadcast([P, NP_, 2, d]),
                                      ALU.mult).then_inc(S["v_done"], 1)
                if a2 is not None:
                    for j in (2, 3):
                        wait(dve, S["scores_ps"], 4 * a2.t + j + 1)
                        wait(dve, S["o_ps"], a2.t)
                        dve.tensor_tensor(s_sb[:, j].rearrange("p g r l -> p (g r) l"), pS[j][:].rearrange("p (n l) -> p n l", l=P),
                                          tri[:].unsqueeze(1).to_broadcast([P, 4, P]), ALU.mult).then_inc(S["masked"], 1)

            dve.wait_ge(S["x_first"], 16)
            pipelined(dve, NT, 2, lead_a, 6, step, lambda: dve.wait_ge(S["x_rest"], 16))

            r = [0]

            def tab(ins):
                r[0] += 1
                ins.then_inc(S["tabs"], 1)
                dve.wait_ge(S["tabs"], r[0])

            dve.wait_ge(S["cnt_ps"], 1)
            tab(dve.tensor_scalar(cnt_i[:], pT1[:, 0:E], float(P - 1), None, ALU.add))
            tab(dve.tensor_scalar(nt_i[:], cnt_i[:], 7, None, ALU.logical_shift_right))
            tab(dve.tensor_copy(ntf[:], nt_i[:]))
            tab(dve.tensor_tensor_scan(endt[:], ones_f[:], ntf[:], 0.0, ALU.mult, ALU.add))
            for n in range(2):
                tab(dve.tensor_scalar(behind[:, n, :], endt[:], jc[:, n:n + 1], None, ALU.is_le))
            tab(dve.tensor_reduce(ej[:], behind[:], AX_X, ALU.add))
            tab(dve.tensor_tensor(bnt[:], behind[:], ntf[:].unsqueeze(1).to_broadcast([P, 2, E]), ALU.mult))
            tab(dve.tensor_reduce(stj[:], bnt[:], AX_X, ALU.add))
            tab(dve.tensor_tensor(jrel[:], jc[:], stj[:], ALU.subtract))
            tab(dve.scalar_tensor_tensor(out=blk[:], in0=ej[:], scalar=float(NBE), in1=jrel[:], op0=ALU.mult, op1=ALU.add))
            tab(dve.tensor_scalar(blk_i[:], blk[:], float(NB), None, ALU.min))
            tab(dve.tensor_scalar(ejc[:], ej[:], float(E - 1), None, ALU.min))
            dve.tensor_copy(jrel[:], jc[:]).then_inc(S["tab_blk"], 1)
            flat_w = wts[:].rearrange("p t k -> p (t k)")
            tab(dve.tensor_scalar(rank_i[:], posi_all[:].rearrange("p t k -> p (t k)"), T - 1, None, ALU.bitwise_and))
            tab(dve.tensor_scalar(inside[:], rank_i[:], float(CAP), None, ALU.is_lt))
            tab(dve.tensor_tensor(flat_w, flat_w, inside[:], ALU.mult))

            tab(dve.memset(shift[:], 0.0))
            tab(dve.tensor_tensor(shift[:, 0:E], endt[:], ntf[:], ALU.subtract))
            tab(dve.scalar_tensor_tensor(out=shift[:, 0:E], in0=shift[:, 0:E], scalar=float(P), in1=ebase[:], op0=ALU.mult,
                                         op1=ALU.subtract))
            flat_pos = posi_all[:].rearrange("p t k -> p (t k)")
            tab(dve.tensor_scalar(place_e[:], flat_pos, T.bit_length() - 1, None, ALU.logical_shift_right))
            tab(dve.tensor_copy(place_ef[:], place_e[:]))
            tab(dve.tensor_copy(rowf[:], flat_pos))
            dve.wait_ge(S["erow_ps"], 1)
            dve.tensor_copy(erow[:], pT1[0:1, 0:256]).then_inc(S["erow_done"], 1)
            dve.wait_ge(S["tab_ps"], 1)
            tab(dve.tensor_copy(slot_i[:], pT0[:, 0:NJ]))
            tab(dve.tensor_scalar(tok_i[:], slot_i[:], 2, None, ALU.logical_shift_right))
            tab(dve.tensor_scalar(tok_i[:], tok_i[:], float(T - 1), None, ALU.min))
            dve.engine_nop().then_inc(S["tab_done"], 1)

            def expert_step(tile_of):
                if (a := tile_of(0)) is not None and a.ring == 0:
                    wait(dve, S["row_tab"], a.turn)
                    dve.tensor_scalar(moved[:], place_ef[:], eidx[:, bass.ds(a.turn, 1)], shift[:, bass.ds(a.turn, 1)],
                                      ALU.is_equal, ALU.mult).then_inc(S["moved_done"], 1)
                if (a := tile_of(0)) is not None and a.ring == 2:
                    wait(dve, S["moved_done"], a.turn + 1)
                    dve.tensor_tensor(rowf[:], rowf[:], moved[:], ALU.add).then_inc(S["row_tab"], 1)
                if (a := tile_of(0)) is not None:
                    wait(dve, gathered[a.ring], (a.t - a.ring) * 4)
                    dve.tensor_copy(tok_b[:, a.ring:a.ring + 1], tok_i[:, bass.ds(a.t, 1)]).then_inc(S["bcopy"], 1)
                if (a := tile_of(6)) is not None:
                    wait(dve, S["gT_ps"], a.t + 1)
                    wait(dve, S["y_ps"], a.t - 1)
                    dve.tensor_copy(geT[:, a.b, :], pT1[:, 0:P]).then_inc(S["gT_done"], 1)
                if (a := tile_of(5)) is not None:
                    wait(dve, S["sge_done"], a.t + 1)
                    wait(dve, S["gT_ps"], a.t - 1)
                    dve.tensor_tensor(ge[:, a.b, :], sge[:, a.b, :], pS[a.b][:, F:2 * F], ALU.mult).then_inc(S["ge_done"], 1)
            pipelined(dve, NJ, 4, lead_b, 8, expert_step)

            tab(dve.tensor_copy(row_i[:].rearrange("p t k -> p (t k)"), rowf[:]))
            QT_ = TG // P
            for t in range(QT_):
                dve.tensor_copy(row_b[:, t, :], row_i[:, t, :]).then_inc(S["rcopy"], 1)

            def group_step(tile_of):
                if (a := tile_of(0)) is not None:
                    for m in range(FC):
                        wait(dve, S["silu_done"], FC * a.t + m + 1)
                        wait(dve, S["z_ps"], QT_ * (a.t - 1))
                        dve.tensor_tensor(gsh[:, a.b, m, :], sg[:, m, :], pS[2 * m + 1][:], ALU.mult).then_inc(S["gsh_done"], 1)
                if (a := tile_of(1)) is not None:
                    for q in range(QT_):
                        t = a.t * QT_ + q
                        xt = xall[:, bass.ds(t, 1), :].rearrange("p a c -> p (a c)")
                        wait(dve, S["z_ps"], t + 1)
                        dve.tensor_tensor(xt, xt, (pQV, pO)[q % 2][:, 0:D], ALU.add).then_inc(S["z_done"], 1)
                        wait(dve, S["z_done"], t + 1)
                        wait(dve, rows_in[q], 16 * TOP_K * (a.t + 1))
                        for k in range(TOP_K):
                            ins = dve.scalar_tensor_tensor(out=xt, in0=rows[:, q, k, :],
                                                           scalar=wts[:, bass.ds(t, 1), k:k + 1].rearrange("p a k -> p (a k)"),
                                                           in1=xt, op0=ALU.mult, op1=ALU.add)
                            if k < TOP_K - 1:
                                ins.then_inc(S["added"], 1)
                                wait(dve, S["added"], (TOP_K - 1) * t + k + 1)
                            else:
                                ins.then_inc(S["summed"], 1)
                        if not (isinstance(t, int) and t + QT_ >= NT):
                            dve.tensor_copy(row_b[:, q, :], row_i[:, bass.ds(t + QT_, 1), :].rearrange("p a k -> p (a k)")
                                            ).then_inc(S["rcopy"], 1)
            pipelined(dve, NG, 2, 2, 1, group_step)


_INS = ["L0_attn_X", "L0_attn_Wq", "L0_attn_Wv", "L0_attn_q_norm_w", "L0_attn_v_norm_w", "L0_ffn_Wg", "L0_ffn_W1",
        "L0_ffn_W2", "L0_ffn_W3", "L0_ffn_Ws1", "L0_ffn_Ws2", "L0_ffn_Ws3"]


def kernel(**inputs):
    import numpy as _np
    import concourse.bacc as _bacc
    from concourse import mybir as _mybir
    from concourse.bass_utils import run_bass_kernel_spmd as _run

    nc = _bacc.Bacc("TRN2", target_bir_lowering=False, num_devices=1)
    arrays, args = {}, []
    for name in _INS:
        a = _np.ascontiguousarray(inputs[name])
        arrays[f"in_{name}"] = a
        args.append(nc.dram_tensor(f"in_{name}", a.shape, _mybir.dt.from_np(a.dtype), kind="ExternalInput").ap())
    shape = inputs["L0_attn_X"].shape
    args.append(nc.dram_tensor("out", shape, _mybir.dt.float32, kind="ExternalOutput").ap())
    build(nc, *args)
    r = _run(nc, [arrays], core_ids=[0])
    return r.results[0]["out"]
```
